# Optimizing a Trainium2 kernel written in Bass

```python
import numpy as np
import jax
import jax.numpy as jnp

def _softmax(x, axis=-1):
    return jax.nn.softmax(x, axis=axis)

def _gelu(x):
    return jax.nn.gelu(x, approximate=True)

def _silu(x):
    return jax.nn.silu(x)

def _sigmoid(x):
    return jax.nn.sigmoid(x)

def _layernorm(x, axis=-1, eps=1e-05):
    m = jnp.mean(x, axis=axis, keepdims=True)
    v = jnp.var(x, axis=axis, keepdims=True)
    return (x - m) / jnp.sqrt(v + eps)

def _scatter_add(tgt, idx, src, axis=0):
    return tgt.at[idx].add(src)

def _segment_sum(src, seg, n):
    return jax.ops.segment_sum(src, seg, n)
kernel_name = 'mk_adj_preln_d4_adj_r2_824bf8'

def setup_inputs(seed: int=0):
    np.random.seed(seed)
    _w = jnp.asarray

    def _rec_inputs():
        import jax
        import jax.numpy as jnp
        _gk = jax.random.key(seed)
        x = -0.000929 + 1 * jax.random.normal(jax.random.fold_in(_gk, 1), (4096, 128), jnp.float32)
        _a = jax.random.bernoulli(jax.random.fold_in(_gk, 2), 0.00195312, (4096, 4096))
        adj = _a.astype(jnp.int32)
        return (x, adj)
    x, adj = _rec_inputs()

    def _L0_gnn_setup():
        import jax, jax.numpy as jnp
        import numpy as np
        from jax import lax
        N = 4096
        D = 128
        CHUNK = 128
        key = jax.random.key(seed)
        k1, k2 = jax.random.split(key)
        x = jax.random.normal(k1, (N, D), dtype=jnp.float32)
        adj = jax.random.randint(k2, (N, N), 0, 2, dtype=jnp.int32)
        return {'x': x, 'adj': adj}
    _L0_gnn_all = _L0_gnn_setup()
    _L0_gnn_in = {k: v for k, v in _L0_gnn_all.items() if k in ()}
    del _L0_gnn_all

    def _L1_gnn_setup():
        import jax, jax.numpy as jnp
        import numpy as np
        N, D_IN, D_OUT = (4096, 128, 128)
        NEG_BIG = 1000000.0
        key = jax.random.key(seed)
        ks = jax.random.split(key, 9)
        s_in = 1.0 / np.sqrt(D_IN)
        s_out = 1.0 / np.sqrt(D_OUT)
        return {'H': jax.random.normal(ks[0], (N, D_IN), dtype=jnp.float32), 'adj': jax.random.randint(ks[1], (N, N), 0, 2, dtype=jnp.int32), 'Wq': jax.random.normal(ks[2], (D_IN, D_OUT), dtype=jnp.float32) * s_in, 'Wk': jax.random.normal(ks[3], (D_IN, D_OUT), dtype=jnp.float32) * s_in, 'Wv': jax.random.normal(ks[4], (D_IN, D_OUT), dtype=jnp.float32) * s_in, 'W1': jax.random.normal(ks[5], (D_OUT, D_OUT), dtype=jnp.float32) * s_out, 'b1': jnp.zeros((D_OUT,), dtype=jnp.float32), 'W2': jax.random.normal(ks[6], (D_OUT, D_OUT), dtype=jnp.float32) * s_out, 'b2': jnp.zeros((D_OUT,), dtype=jnp.float32)}
    _L1_gnn_all = _L1_gnn_setup()
    _L1_gnn_in = {k: v for k, v in _L1_gnn_all.items() if k in ('Wq', 'Wk', 'Wv', 'W1', 'b1', 'W2', 'b2')}
    del _L1_gnn_all

    def _L2_gnn_setup():
        import jax, jax.numpy as jnp
        import numpy as np
        NEG_INF = -9000000000000000.0
        LEAKY_SLOPE = 0.2
        key = jax.random.key(seed)
        k1, k2, k3, k4 = jax.random.split(key, 4)
        N, dim = (2048, 128)
        hidden = jax.random.normal(k1, (N, dim), dtype=jnp.float32)
        adj = jax.random.randint(k2, (N, N), 0, 5)
        W = jax.random.normal(k3, (4, dim), dtype=jnp.float32) * (1.0 / np.sqrt(dim))
        b = jax.random.normal(k4, (4,), dtype=jnp.float32) * 0.01
        return {'hidden': hidden, 'adj': adj, 'W': W, 'b': b}
    _L2_gnn_all = _L2_gnn_setup()
    _L2_gnn_in = {k: v for k, v in _L2_gnn_all.items() if k in ('W', 'b')}
    del _L2_gnn_all

    def _L3_gnn_setup():
        import jax, jax.numpy as jnp
        import numpy as np
        N = 4096
        D_IN = 128
        D_OUT = 128
        ALPHA = 0.2
        NEG = -9000000000000000.0
        key = jax.random.key(seed)
        k1, k2, k3, k4 = jax.random.split(key, 4)
        input = jax.random.normal(k1, (N, D_IN), dtype=jnp.float32)
        adj = jax.random.randint(k2, (N, N), 0, 2, dtype=jnp.int32)
        lim_w = 1.414 * np.sqrt(6.0 / (D_IN + D_OUT))
        W = jax.random.uniform(k3, (D_IN, D_OUT), jnp.float32, -lim_w, lim_w)
        lim_a = 1.414 * np.sqrt(6.0 / (2 * D_OUT + 1))
        a = jax.random.uniform(k4, (2 * D_OUT, 1), jnp.float32, -lim_a, lim_a)
        return {'input': input, 'adj': adj, 'W': W, 'a': a}
    _L3_gnn_all = _L3_gnn_setup()
    _L3_gnn_in = {k: v for k, v in _L3_gnn_all.items() if k in ('W', 'a')}
    del _L3_gnn_all
    return {'x': x, 'adj': adj, 'L1_gnn_Wq': _L1_gnn_in['Wq'], 'L1_gnn_Wk': _L1_gnn_in['Wk'], 'L1_gnn_Wv': _L1_gnn_in['Wv'], 'L1_gnn_W1': _L1_gnn_in['W1'], 'L1_gnn_b1': _L1_gnn_in['b1'], 'L1_gnn_W2': _L1_gnn_in['W2'], 'L1_gnn_b2': _L1_gnn_in['b2'], 'L2_gnn_W': _L2_gnn_in['W'], 'L2_gnn_b': _L2_gnn_in['b'], 'L3_gnn_W': _L3_gnn_in['W'], 'L3_gnn_a': _L3_gnn_in['a']}

def reference(x, adj, L1_gnn_Wq, L1_gnn_Wk, L1_gnn_Wv, L1_gnn_W1, L1_gnn_b1, L1_gnn_W2, L1_gnn_b2, L2_gnn_W, L2_gnn_b, L3_gnn_W, L3_gnn_a):
    import jax
    import jax.numpy as jnp

    def _L0_gnn_ref(x, adj):
        import jax, jax.numpy as jnp
        import numpy as np
        from jax import lax
        N = 4096
        D = 128
        CHUNK = 128
        n, d = x.shape
        neg = jnp.finfo(x.dtype).min
        adj_chunks = adj.reshape(n // CHUNK, CHUNK, n)

        def step(carry, a):
            mask = a != 0
            masked = jnp.where(mask[:, :, None], x[None, :, :], neg)
            m = jnp.max(masked, axis=1)
            has_nbr = jnp.any(mask, axis=1)
            out = jnp.where(has_nbr[:, None], m, jnp.zeros((), x.dtype))
            return (carry, out)
        _, out = lax.scan(step, None, adj_chunks)
        return out.reshape(n, d)

    def _L1_gnn_ref(H, adj, Wq, Wk, Wv, W1, b1, W2, b2):
        import jax, jax.numpy as jnp
        import numpy as np
        N, D_IN, D_OUT = (4096, 128, 128)
        NEG_BIG = 1000000.0
        q = H @ Wq
        k = H @ Wk
        v = H @ Wv
        scores = q @ k.T
        att_mask = (adj > 0).astype(scores.dtype)
        masked_scores = scores - (1.0 - att_mask) * NEG_BIG
        att = jax.nn.softmax(masked_scores, axis=-1)
        M = att @ v
        h = jax.nn.relu(M @ W1 + b1)
        out = jax.nn.relu(h @ W2 + b2)
        return out

    def _L2_gnn_ref(hidden, adj, W, b):
        import jax, jax.numpy as jnp
        import numpy as np
        NEG_INF = -9000000000000000.0
        LEAKY_SLOPE = 0.2
        hw = hidden[None, :, :] * W[:, None, :]
        e = jnp.einsum('knd,md->knm', hw, hidden) + b[:, None, None]
        e = jax.nn.leaky_relu(e, negative_slope=LEAKY_SLOPE)
        neg = jnp.asarray(NEG_INF, dtype=e.dtype)
        alpha = jnp.where(adj == 1, e[0], neg)
        alpha = jnp.where(adj == 2, e[1], alpha)
        alpha = jnp.where(adj == 3, e[2], alpha)
        alpha = jnp.where(adj == 4, e[3], alpha)
        alpha = jax.nn.softmax(alpha, axis=-1)
        return alpha @ hidden

    def _L3_gnn_ref(input, adj, W, a):
        import jax, jax.numpy as jnp
        import numpy as np
        N = 4096
        D_IN = 128
        D_OUT = 128
        ALPHA = 0.2
        NEG = -9000000000000000.0
        h = input @ W
        a1 = a[:D_OUT, 0]
        a2 = a[D_OUT:, 0]
        e = (h @ a1)[:, None] + (h @ a2)[None, :]
        e = jnp.where(e > 0, e, ALPHA * e)
        e = jnp.where(adj > 0, e, NEG)
        attention = jax.nn.softmax(e, axis=1)
        h_prime = attention @ h
        return jax.nn.elu(h_prime)
    h = jnp.maximum(_layernorm(x, axis=-1), 0.0)
    x = x + _L0_gnn_ref(h, adj)
    h = jnp.maximum(_layernorm(x, axis=-1), 0.0)
    x = x + _L1_gnn_ref(h, adj, L1_gnn_Wq, L1_gnn_Wk, L1_gnn_Wv, L1_gnn_W1, L1_gnn_b1, L1_gnn_W2, L1_gnn_b2)
    h = jnp.maximum(_layernorm(x, axis=-1), 0.0)
    x = x + _L2_gnn_ref(h, adj, L2_gnn_W, L2_gnn_b)
    h = jnp.maximum(_layernorm(x, axis=-1), 0.0)
    x = x + _L3_gnn_ref(h, adj, L3_gnn_W, L3_gnn_a)
    return x

_drawn_inputs = setup_inputs


def setup_inputs(seed=0):
    import zlib

    import numpy as np

    out = dict(_drawn_inputs(seed))
    spreads = {'L1_gnn_b1': (0.0, 0.354), 'L1_gnn_b2': (0.0, 0.1)}
    factors = {'L2_gnn_b': 8.0}
    for name, (base, spread) in spreads.items():
        noise = np.random.default_rng([zlib.crc32(name.encode()), seed]).standard_normal(out[name].shape)
        drawn = base * np.exp(spread * noise) if base else spread * noise
        out[name] = jnp.asarray(drawn.astype(out[name].dtype))
    for name, factor in factors.items():
        out[name] = (out[name] * factor).astype(out[name].dtype)
    return out
```

```python
from contextlib import ExitStack, contextmanager

import concourse.bass as bass
from concourse import mybir

F32 = mybir.dt.float32
BF16 = mybir.dt.bfloat16
I32 = mybir.dt.int32
ALU = mybir.AluOpType
ACT = mybir.ActivationFunctionType
AX = mybir.AxisListType

P = 128
LN_EPS = 1e-5
NEG_BIG = 1.0e6
NEG_INF = -9.0e15
SLOPE = 0.2
HEADS = 4
LAYERS = 4


class Chain:

    def __init__(self, eng, sem):
        self.eng, self.sem, self.n = eng, sem, 0

    def __call__(self, ins):
        ins.then_inc(self.sem, 1)
        self.n = self.n + 1
        self.eng.wait_ge(self.sem, self.n)

    @contextmanager
    def loop(self, count, steps):
        start = self.n
        with self.eng.Fori(0, count) as i:
            self.n = start + i * steps
            yield i
        self.n = start + count * steps


def build(nc, x, adj, Wq, Wk, Wv, W1, b1, W2, b2, W2h, b2h, W3, a3, out):
    N, D = x.shape
    T = N // P
    CH = N // 512
    Q = N // 1024
    x_rows = x.rearrange("(t p) d -> p t d", p=P)
    out_rows = out.rearrange("(t p) d -> p t d", p=P)

    with ExitStack() as ctx:
        def sb(name, shape, dt=F32):
            return ctx.enter_context(nc.sbuf_tensor(name, shape, dt))

        def pb(name, shape):
            return ctx.enter_context(nc.psum_tensor(name, shape, F32))

        def sem(name):
            return ctx.enter_context(nc.semaphore(name))

        wq, wk, wv, w1, w2, w3 = (sb(n, [P, D]) for n in ("wq", "wk", "wv", "w1", "w2", "w3"))
        wT = sb("wT", [P, 4, D])
        a_cols = sb("a_cols", [P, 2])
        b1_col = sb("b1_col", [P, 1])
        b2_rows = sb("b2_rows", [P, D])
        head_cols = sb("head_cols", [P, HEADS])
        head_bias = sb("head_bias", [P, HEADS])
        w_qk = sb("w_qk", [P, D])
        w_v1 = sb("w_v1", [P, D])
        w_a = sb("w_a", [P, 2])
        w_a2 = sb("w_a2", [P, P])
        ones = sb("ones", [P, P])
        ident = sb("ident", [P, P])
        ident_b = sb("ident_b", [P, P], BF16)

        xs = sb("xs", [P, T, D])
        hs = sb("hs", [P, T, D])
        hT = sb("hT", [P, N])
        stats = sb("stats", [P, T, 6])
        mean, gap, var = sb("mean", [P, T]), sb("gap", [P, T]), sb("var", [P, T])
        std, rstd, shift = sb("std", [P, T]), sb("rstd", [P, T]), sb("shift", [P, T])
        h_tile = sb("h_tile", [P, D])
        u_tile = sb("u_tile", [P, D])
        uT_tile = sb("uT_tile", [P, P])
        hid_tile = sb("hid_tile", [P, P])
        sum_tile = sb("sum_tile", [P, D])
        max_col = sb("max_col", [P, 1])
        negmax = sb("negmax", [P, 1])
        denom = sb("denom", [P, 1])
        rdenom = sb("rdenom", [P, 1])

        adj_tile = sb("adj_tile", [P, N], I32)
        scores = sb("scores", [P, N])
        probs = sb("probs", [P, N])
        mask_b = sb("mask_b", [P, N], BF16)
        chunk_a = sb("chunk_a", [P, 1024])
        chunk_b = sb("chunk_b", [P, 512])
        pT = sb("pT", [P, 2, 512])
        queries = sb("queries", [P, HEADS, P])
        f1_col = sb("f1_col", [P, 1])
        quarter_max = sb("quarter_max", [P, Q])
        maxT = sb("maxT", [P, P])

        ps_big = pb("ps_big", [P, 4, 512])
        ps_t = pb("ps_t", [P, 512])
        ps_acc = pb("ps_acc", [P, 512])
        ps_e = pb("ps_e", [P, 512])
        ps_f = pb("ps_f", [P, 512])

        x_in = sem("x_in")
        weights_in = sem("weights_in")
        ident_zeroed = sem("ident_zeroed")
        ident_ready = sem("ident_ready")
        wT_ready = sem("wT_ready")
        wT_copied = sem("wT_copied")
        products_ready = sem("products_ready")
        products_copied = sem("products_copied")
        dve_step = sem("dve_step")
        out_done = sem("out_done")

        def sems(name):
            return [sem(f"{name}{layer}") for layer in range(LAYERS)]

        norm_ready = sems("norm_ready")
        h_ready = sems("h_ready")
        var_ready = sems("var_ready")
        std_ready = sems("std_ready")
        hT_ready = sems("hT_ready")
        h_stored = sems("h_stored")
        adj_in = sems("adj_in")
        adj_free = sems("adj_free")
        u_ready = sems("u_ready")
        uT_ready = sems("uT_ready")
        uT_copied = sems("uT_copied")
        hid_ready = sems("hid_ready")
        hid_copied = sems("hid_copied")
        delta_ready = sems("delta_ready")
        elu_in = sems("elu_in")
        elu_exp = sems("elu_exp")
        x_updated = sems("x_updated")
        mask_ready = sem("mask_ready")
        quarters_ready = sem("quarters_ready")
        quarters_used = sem("quarters_used")
        maxT_ready = sem("maxT_ready")
        max_ready = sem("max_ready")
        row_max_taken = sem("row_max_taken")
        u_copied = sems("u_copied")
        lhs_made = sems("lhs_made")
        lhs_product = sems("lhs_product")
        lhs_ready = sems("lhs_ready")
        banks_ready = sems("banks_ready")
        banks_used = sems("banks_used")
        rowmax_ready = sems("rowmax_ready")
        probs_ready = sems("probs_ready")
        pT_ready = sems("pT_ready")
        pT_copied = sems("pT_copied")
        pv_done = sems("pv_done")

        block = ctx.enter_context(nc.Block())
        WEIGHTS = 16 * 12
        heads = [0, 1, HEADS, 1]

        @block.sync
        def _(sp):
            sp.dma_start(xs[:, :, :], x_rows).then_inc(x_in, 16)
            for dst, src in ((wq, Wq), (wk, Wk), (wv, Wv), (w1, W1), (w2, W2), (w3, W3)):
                sp.dma_start(dst[:, :], src).then_inc(weights_in, 16)
            for c in range(2):
                sp.dma_start(a_cols[:, c:c + 1], a3[c * D:(c + 1) * D, :]).then_inc(weights_in, 16)
            sp.dma_start(b1_col[:, :], b1.rearrange("(p o) -> p o", o=1)).then_inc(weights_in, 16)
            sp.dma_start(b2_rows[:, :], b2.partition_broadcast(P)).then_inc(weights_in, 16)
            sp.dma_start(head_cols[:, :], W2h.rearrange("k d -> d k"), allow_slow_non_contiguous=True).then_inc(weights_in, 16)
            sp.dma_start(head_bias[:, :], b2h.partition_broadcast(P)).then_inc(weights_in, 16)
            for layer in range(LAYERS):
                if layer:
                    sp.wait_ge(adj_free[layer - 1], T)
                sp.dma_start(adj_tile[:, :], adj[0:P, :]).then_inc(adj_in[layer], 16)
                with sp.Fori(1, T) as t:
                    sp.wait_ge(adj_free[layer], t)
                    sp.dma_start(adj_tile[:, :], adj[bass.ds(t * P, P), :]).then_inc(adj_in[layer], 16)
            sp.wait_ge(x_updated[LAYERS - 1], T)
            sp.dma_start(out_rows, xs[:, :, :]).then_inc(out_done, 16)
            sp.wait_ge(out_done, 16)

        @block.gpsimd
        def _(pool):
            pool.memset(ident[:, :], 0.0).then_inc(ident_zeroed, 1)
            pool.memset(ident_b[:, :], 0.0).then_inc(ident_zeroed, 1)
            pool.memset(ones[:, :], 1.0).then_inc(ident_ready, 1)
            pool.wait_ge(ident_zeroed, 2)
            for m in (ident, ident_b):
                pool.affine_select(out=m[:, :], in_=m[:, :], compare_op=ALU.not_equal, fill=1.0, base=0,
                                   pattern=[[-1, P]], channel_multiplier=1).then_inc(ident_ready, 1)

        @block.tensor
        def _(pe):
            pe.wait_ge(ident_ready, 3)
            pe.wait_ge(weights_in, WEIGHTS)
            for i, w in enumerate((wq, wk, wv, w3)):
                mm = pe.transpose(ps_t[:, i * P:(i + 1) * P], w[:, :], ident[:, :])
            mm.then_inc(wT_ready, 1)
            pe.wait_ge(wT_copied, 1)
            pe.matmul(ps_e[:, 0:D], wT[:, 0, :], wT[:, 1, :], start=True, stop=True)
            pe.matmul(ps_acc[:, 0:D], wT[:, 2, :], w1[:, :], start=True, stop=True)
            pe.matmul(ps_f[:, 0:2], wT[:, 3, :], a_cols[:, :], start=True, stop=True).then_inc(products_ready, 1)
            pe.wait_ge(products_copied, 1)

            def transpose_rows(layer):
                with pe.Fori(0, T) as t:
                    pe.wait_ge(h_ready[layer], t + 1)
                    pe.transpose(ps_t[:, 0:P], h_tile[:, :], ident[:, :]).then_inc(hT_ready[layer], 1)
                pe.wait_ge(h_stored[layer], T + 1)

            def finish(layer, n):
                if layer == 2:
                    return
                pe.wait_ge(u_ready[layer], n + 1)
                pe.transpose(ps_e[:, 0:P], u_tile[:, :], ident[:, :]).then_inc(uT_ready[layer], 1)
                pe.wait_ge(uT_copied[layer], n + 1)
                if layer == 1:
                    pe.matmul(ps_f[:, 0:P], w_v1[:, :], uT_tile[:, :], start=True, stop=True).then_inc(hid_ready[layer], 1)
                    pe.wait_ge(hid_copied[layer], n + 1)
                    pe.matmul(ps_e[:, 0:D], hid_tile[:, :], w2[:, :], start=True, stop=True).then_inc(delta_ready[layer], 1)
                else:
                    pe.matmul(ps_f[:, 0:D], uT_tile[:, :], w3[:, :], start=True, stop=True).then_inc(delta_ready[layer], 1)

            transpose_rows(0)
            with pe.Fori(0, T) as t:
                with pe.Fori(0, P) as r:
                    pe.wait_ge(mask_ready, t + 1)
                    for q in range(Q):
                        pe.wait_ge(quarters_used, (t * P + r) * Q + q + 1)
                        for half in range(2):
                            c = 2 * q + half
                            mm = pe.matmul(ps_big[:, 2 * (q % 2) + half, :],
                                           ident_b[:, bass.ds(r, 1)].to_broadcast([P, P]),
                                           mask_b[:, c * 512:(c + 1) * 512], start=True, stop=True)
                        mm.then_inc(quarters_ready, 1)
                pe.wait_ge(maxT_ready, t + 1)
                pe.transpose(ps_t[:, 0:P], maxT[:, :], ident[:, :]).then_inc(max_ready, 1)

            for layer in range(1, LAYERS):
                transpose_rows(layer)
                with pe.Fori(0, T) as t:
                    if layer == 1:
                        pe.matmul(ps_t[:, 0:P], w_qk[:, :], hT[:, bass.ds(t * P, P)], start=True,
                                  stop=True).then_inc(lhs_product[layer], 1)
                    if layer == 3:
                        pe.wait_ge(lhs_made[layer], t + 1)
                        pe.matmul(ps_t[:, 0:1], queries[:, 0, :], w_a[:, 0:1], start=True,
                                  stop=True).then_inc(lhs_product[layer], 1)
                    pe.wait_ge(lhs_ready[layer], t + 1)
                    banks = CH * heads[layer]
                    for i in range(banks):
                        c, k = divmod(i, heads[layer])
                        pe.wait_ge(banks_used[layer], t * banks + i + 1)
                        pe.matmul(ps_big[:, i % 2, :], w_a2[:, :] if layer == 3 else queries[:, k, :],
                                  hT[:, c * 512:(c + 1) * 512], start=True, stop=True).then_inc(banks_ready[layer], 1)
                    pe.wait_ge(probs_ready[layer], t + 1)
                    for c in range(CH + 1):
                        if c < CH:
                            if c >= 2:
                                pe.wait_ge(pT_copied[layer], t * CH + c - 1)
                            for b in range(4):
                                j = c * 4 + b
                                mm = pe.transpose(ps_big[:, 2 + c % 2, b * P:(b + 1) * P],
                                                  probs[:, j * P:(j + 1) * P], ident[:, :])
                            mm.then_inc(pT_ready[layer], 1)
                        if c:
                            pe.wait_ge(pT_copied[layer], t * CH + c)
                            for b in range(4):
                                j = (c - 1) * 4 + b
                                mm = pe.matmul(ps_acc[:, 0:D], pT[:, (c - 1) % 2, b * P:(b + 1) * P], hs[:, j, :],
                                               start=(j == 0), stop=(j == T - 1))
                            mm.then_inc(pv_done[layer], 1)
                    finish(layer, t)

        @block.scalar
        def _(act):
            def normalise(layer):
                act.wait_ge(var_ready[layer], 1)
                act.activation(std[:, :], var[:, :], ACT.Sqrt).then_inc(std_ready[layer], 1)
                act.wait_ge(norm_ready[layer], 1)
                with act.Fori(0, T) as t:
                    act.wait_ge(h_stored[layer], t + 1)
                    act.activation(h_tile[:, :], xs[:, bass.ds(t, 1), :].rearrange("p o d -> p (o d)"), ACT.Relu,
                                   bias=shift[:, bass.ds(t, 1)], scale=rstd[:, bass.ds(t, 1)]).then_inc(h_ready[layer], 1)

            def finish(layer, n):
                if layer == 1:
                    act.wait_ge(hid_ready[layer], n + 1)
                    act.activation(hid_tile[:, :], ps_f[:, 0:P], ACT.Relu, bias=b1_col[:, :]).then_inc(hid_copied[layer], 1)
                if layer == 3:
                    act.wait_ge(elu_in[layer], n + 1)
                    act.activation(hid_tile[:, :], sum_tile[:, :], ACT.Exp).then_inc(elu_exp[layer], 1)

            act.wait_ge(weights_in, WEIGHTS)
            normalise(0)
            for layer in range(1, LAYERS):
                normalise(layer)
                with act.Fori(0, T) as t:
                    act.wait_ge(rowmax_ready[layer], t + 1)
                    act.activation(probs[:, :], scores[:, :], ACT.Exp, bias=negmax[:, :],
                                   accum_out=denom[:, :]).then_inc(probs_ready[layer], 1)
                    for c in range(CH):
                        act.wait_ge(pT_ready[layer], t * CH + c + 1)
                        if c >= 2:
                            act.wait_ge(pv_done[layer], t * CH + c - 1)
                        act.activation(pT[:, c % 2, :], ps_big[:, 2 + c % 2, :], ACT.Copy).then_inc(pT_copied[layer], 1)
                    finish(layer, t)

        @block.vector
        def _(dve):
            step = Chain(dve, dve_step)

            def row_tile(a, t):
                return a[:, bass.ds(t, 1), :].rearrange("p o d -> p (o d)")

            dve.wait_ge(ident_ready, 3)
            dve.wait_ge(wT_ready, 1)
            dve.tensor_copy(wT[:, :, :].rearrange("p a d -> p (a d)"), ps_t[:, :]).then_inc(wT_copied, 1)
            dve.wait_ge(products_ready, 1)
            step(dve.tensor_copy(w_qk[:, :], ps_e[:, 0:D]))
            step(dve.tensor_copy(w_v1[:, :], ps_acc[:, 0:D]))
            step(dve.tensor_copy(w_a[:, :], ps_f[:, 0:2]))
            dve.tensor_scalar(w_a2[:, :], ones[:, :], w_a[:, 1:2], None, ALU.mult).then_inc(products_copied, 1)
            dve.wait_ge(x_in, 16)

            def layer_stats(layer):
                even_mean, even_m2, odd_mean, odd_m2 = (stats[:, :, i] for i in (1, 2, 4, 5))
                step(dve.tensor_tensor(mean[:, :], even_mean, odd_mean, ALU.add))
                step(dve.tensor_tensor(gap[:, :], even_mean, odd_mean, ALU.subtract))
                step(dve.tensor_tensor(var[:, :], even_m2, odd_m2, ALU.add))
                step(dve.tensor_tensor(gap[:, :], gap[:, :], gap[:, :], ALU.mult))
                step(dve.scalar_tensor_tensor(out=var[:, :], in0=gap[:, :], scalar=D / 4.0, in1=var[:, :],
                                              op0=ALU.mult, op1=ALU.add))
                dve.tensor_scalar(var[:, :], var[:, :], 1.0 / D, LN_EPS, ALU.mult, ALU.add).then_inc(var_ready[layer], 1)
                dve.wait_ge(std_ready[layer], 1)
                step(dve.reciprocal(rstd[:, :], std[:, :]))
                dve.scalar_tensor_tensor(out=shift[:, :], in0=mean[:, :], scalar=-0.5, in1=rstd[:, :],
                                         op0=ALU.mult, op1=ALU.mult).then_inc(norm_ready[layer], 1)

            def normalise(layer):
                with step.loop(T, 1) as t:
                    step(dve.bn_stats(row_tile(stats, t), row_tile(xs, t)))
                layer_stats(layer)
                dve.sem_inc(h_stored[layer], 1)
                with dve.Fori(0, T) as t:
                    dve.wait_ge(h_ready[layer], t + 1)
                    dve.tensor_copy(row_tile(hs, t), h_tile[:, :])
                    dve.wait_ge(hT_ready[layer], t + 1)
                    dve.tensor_copy(hT[:, bass.ds(t * P, P)], ps_t[:, 0:P]).then_inc(h_stored[layer], 1)
                    dve.wait_ge(h_stored[layer], t + 2)

            def finish(layer, n, x_tile):
                if layer == 2:
                    dve.scalar_tensor_tensor(out=x_tile, in0=u_tile[:, :], scalar=rdenom[:, :], in1=x_tile,
                                             op0=ALU.mult, op1=ALU.add).then_inc(x_updated[layer], 1)
                    dve.wait_ge(x_updated[layer], n + 1)
                    return
                dve.tensor_scalar(u_tile[:, :], u_tile[:, :], rdenom[:, :], None, ALU.mult).then_inc(u_ready[layer], 1)
                dve.wait_ge(uT_ready[layer], n + 1)
                dve.tensor_copy(uT_tile[:, :], ps_e[:, 0:P]).then_inc(uT_copied[layer], 1)
                dve.wait_ge(delta_ready[layer], n + 1)
                if layer == 1:
                    step(dve.tensor_tensor(sum_tile[:, :], ps_e[:, 0:D], b2_rows[:, :], ALU.add))
                    dve.scalar_tensor_tensor(out=x_tile, in0=sum_tile[:, :], scalar=0.0, in1=x_tile,
                                             op0=ALU.max, op1=ALU.add).then_inc(x_updated[layer], 1)
                else:
                    dve.tensor_scalar(sum_tile[:, :], ps_f[:, 0:D], 0.0, None, ALU.min).then_inc(elu_in[layer], 1)
                    dve.wait_ge(elu_exp[layer], n + 1)
                    step(dve.tensor_scalar(hid_tile[:, :], hid_tile[:, :], -1.0, None, ALU.add))
                    step(dve.scalar_tensor_tensor(out=sum_tile[:, :], in0=ps_f[:, 0:D], scalar=0.0,
                                                  in1=hid_tile[:, :], op0=ALU.max, op1=ALU.add))
                    dve.tensor_tensor(x_tile, x_tile, sum_tile[:, :], ALU.add).then_inc(x_updated[layer], 1)
                dve.wait_ge(x_updated[layer], n + 1)

            normalise(0)
            dve.sem_inc(quarters_used, 2)
            with step.loop(T, P * Q) as t:
                dve.wait_ge(adj_in[0], 16 * (t + 1))
                dve.tensor_scalar(mask_b[:, :], adj_tile[:, :], 0.0, None, ALU.not_equal).then_inc(mask_ready, 1)
                dve.wait_ge(mask_ready, t + 1)
                dve.sem_inc(adj_free[0], 1)
                with step.loop(P, Q) as r:
                    for q in range(Q):
                        dve.wait_ge(quarters_ready, (t * P + r) * Q + q + 1)
                        dve.tensor_tensor(chunk_a[:, :],
                                          ps_big[:, 2 * (q % 2):2 * (q % 2) + 2, :].rearrange("p a b -> p (a b)"),
                                          hT[:, q * 1024:(q + 1) * 1024], ALU.mult).then_inc(quarters_used, 1)
                        dve.wait_ge(quarters_used, (t * P + r) * Q + q + 3)
                        step(dve.tensor_reduce(quarter_max[:, q:q + 1], chunk_a[:, :], AX.X, ALU.max))
                    dve.tensor_reduce(maxT[:, bass.ds(r, 1)], quarter_max[:, :], AX.X, ALU.max).then_inc(row_max_taken, 1)
                    dve.wait_ge(row_max_taken, t * P + r + 1)
                dve.sem_inc(maxT_ready, 1)
                dve.wait_ge(max_ready, t + 1)
                dve.tensor_tensor(row_tile(xs, t), row_tile(xs, t), ps_t[:, 0:P], ALU.add).then_inc(x_updated[0], 1)
                dve.wait_ge(x_updated[0], t + 1)

            def dense_scores(layer, t):
                hT_tile = hT[:, bass.ds(t * P, P)]
                banks = CH * heads[layer]
                if layer == 1:
                    dve.wait_ge(lhs_product[layer], t + 1)
                    dve.tensor_copy(queries[:, 0, :], ps_t[:, 0:P]).then_inc(lhs_ready[layer], 1)
                    dve.wait_ge(adj_in[layer], 16 * (t + 1))
                    step(dve.tensor_scalar(scores[:, :], adj_tile[:, :], 0.0, -NEG_BIG, ALU.is_le, ALU.mult))
                    for c in range(CH):
                        part = scores[:, c * 512:(c + 1) * 512]
                        dve.wait_ge(banks_ready[layer], t * banks + c + 1)
                        dve.tensor_tensor(part, part, ps_big[:, c % 2, :], ALU.add).then_inc(banks_used[layer], 1)
                    dve.wait_ge(banks_used[layer], (t + 1) * banks + 2)
                if layer == 2:
                    for k in range(HEADS):
                        ins = dve.tensor_scalar(queries[:, k, :], hT_tile, head_cols[:, k:k + 1], None, ALU.mult)
                    ins.then_inc(lhs_ready[layer], 1)
                    dve.wait_ge(adj_in[layer], 16 * (t + 1))
                    step(dve.tensor_scalar(scores[:, :], adj_tile[:, :], 1.0, None, ALU.is_ge))
                    step(dve.scalar_tensor_tensor(out=scores[:, :], in0=adj_tile[:, :], scalar=float(HEADS),
                                                  in1=scores[:, :], op0=ALU.is_le, op1=ALU.mult))
                    step(dve.tensor_scalar(scores[:, :], scores[:, :], -1.0, -NEG_INF, ALU.add, ALU.mult))
                    for i in range(banks):
                        c, k = divmod(i, HEADS)
                        part = scores[:, c * 512:(c + 1) * 512]
                        dve.wait_ge(banks_ready[layer], t * banks + i + 1)
                        dve.tensor_scalar(chunk_b[:, :], ps_big[:, i % 2, :], head_bias[:, k:k + 1], None,
                                          ALU.add).then_inc(banks_used[layer], 1)
                        dve.wait_ge(banks_used[layer], t * banks + i + 3)
                        step(dve.scalar_tensor_tensor(out=chunk_a[:, 0:512], in0=chunk_b[:, :], scalar=SLOPE,
                                                      in1=chunk_b[:, :], op0=ALU.mult, op1=ALU.max))
                        step(dve.scalar_tensor_tensor(out=chunk_b[:, :], in0=adj_tile[:, c * 512:(c + 1) * 512],
                                                      scalar=float(k + 1), in1=chunk_a[:, 0:512],
                                                      op0=ALU.is_equal, op1=ALU.mult))
                        step(dve.tensor_tensor(part, part, chunk_b[:, :], ALU.add))
                if layer == 3:
                    dve.tensor_copy(queries[:, 0, :], hT_tile).then_inc(lhs_made[layer], 1)
                    dve.wait_ge(lhs_product[layer], t + 1)
                    dve.tensor_copy(f1_col[:, :], ps_t[:, 0:1]).then_inc(lhs_ready[layer], 1)
                    dve.wait_ge(lhs_ready[layer], t + 1)
                    dve.wait_ge(adj_in[layer], 16 * (t + 1))
                    step(dve.tensor_scalar(scores[:, :], adj_tile[:, :], 0.0, NEG_INF, ALU.is_le, ALU.mult))
                    for c in range(CH):
                        part = scores[:, c * 512:(c + 1) * 512]
                        dve.wait_ge(banks_ready[layer], t * banks + c + 1)
                        dve.tensor_scalar(chunk_b[:, :], ps_big[:, c % 2, :], f1_col[:, :], None,
                                          ALU.add).then_inc(banks_used[layer], 1)
                        dve.wait_ge(banks_used[layer], t * banks + c + 3)
                        step(dve.scalar_tensor_tensor(out=chunk_a[:, 0:512], in0=chunk_b[:, :], scalar=SLOPE,
                                                      in1=chunk_b[:, :], op0=ALU.mult, op1=ALU.max))
                        step(dve.scalar_tensor_tensor(out=chunk_b[:, :], in0=adj_tile[:, c * 512:(c + 1) * 512],
                                                      scalar=0.0, in1=chunk_a[:, 0:512], op0=ALU.is_gt, op1=ALU.mult))
                        step(dve.tensor_tensor(part, part, chunk_b[:, :], ALU.add))

            STEPS = [0, 1 + 1, 3 + 3 * CH * HEADS + 1, 1 + 3 * CH + 1]
            FINISH = [0, 1, 0, 2]
            for layer in range(1, LAYERS):
                normalise(layer)
                dve.sem_inc(banks_used[layer], 2)
                with step.loop(T, STEPS[layer] + FINISH[layer] + 1) as t:
                    dense_scores(layer, t)
                    step(dve.tensor_reduce(max_col[:, :], scores[:, :], AX.X, ALU.max))
                    dve.tensor_scalar(negmax[:, :], max_col[:, :], -1.0, None, ALU.mult).then_inc(rowmax_ready[layer], 1)
                    dve.sem_inc(adj_free[layer], 1)
                    dve.wait_ge(probs_ready[layer], t + 1)
                    step(dve.reciprocal(rdenom[:, :], denom[:, :]))
                    dve.wait_ge(pv_done[layer], (t + 1) * CH)
                    dve.tensor_copy(u_tile[:, :], ps_acc[:, 0:D]).then_inc(u_copied[layer], 1)
                    dve.wait_ge(u_copied[layer], t + 1)
                    finish(layer, t, row_tile(xs, t))


_INS = ['x', 'adj', 'L1_gnn_Wq', 'L1_gnn_Wk', 'L1_gnn_Wv', 'L1_gnn_W1', 'L1_gnn_b1', 'L1_gnn_W2', 'L1_gnn_b2',
        'L2_gnn_W', 'L2_gnn_b', 'L3_gnn_W', 'L3_gnn_a']
_OUTS = [((4096, 128), 'float32')]


def kernel(**inputs):
    import numpy as _np
    import concourse.bacc as _bacc
    from concourse import mybir as _mybir
    from concourse.bass_utils import run_bass_kernel_spmd as _run

    nc = _bacc.Bacc("TRN2", target_bir_lowering=False, num_devices=1)
    arrays, args = {}, []
    for name in _INS:
        a = _np.ascontiguousarray(inputs[name])
        arrays[f"in_{name}_dram"] = a
        args.append(nc.dram_tensor(f"in_{name}_dram", a.shape, _mybir.dt.from_np(a.dtype), kind="ExternalInput").ap())
    for i, (shape, dtype) in enumerate(_OUTS):
        dt = _mybir.dt.from_np(_np.dtype(dtype))
        args.append(nc.dram_tensor(f"out_{i}_dram", shape, dt, kind="ExternalOutput").ap())
    build(nc, *args)
    r = _run(nc, [arrays], core_ids=[0])
    got = tuple(r.results[0][f"out_{i}_dram"] for i in range(len(_OUTS)))
    return got[0]
```

```python
from contextlib import ExitStack, contextmanager

import concourse.bass as bass
from concourse import mybir

F32 = mybir.dt.float32
BF16 = mybir.dt.bfloat16
I32 = mybir.dt.int32
U32 = mybir.dt.uint32
ALU = mybir.AluOpType
ACT = mybir.ActivationFunctionType
AX = mybir.AxisListType

P = 128
LN_EPS = 1e-5
NEG_BIG = 1.0e6
NEG_INF = -9.0e15
SLOPE = 0.2
HEADS = 4
LAYERS = 4
SLOTS = 24
GROUP = 512
TOP = 8
PAD_BIAS = -1.0e30
RUNS = [(0, 23), (1, 15), (2, 13), (4, 12), (8, 10), (16, 8), (20, 7), (24, 6)]
W_NODE = SLOTS
W_X = 32


def wait_alone(eng, sem, value, passed):
    eng.wait_ge(sem, value)
    eng.sem_inc(passed, 1)


class Chain:

    def __init__(self, eng, sem):
        self.eng, self.sem, self.n, self.steps = eng, sem, 0, 0

    def __call__(self, ins, passed=None):
        ins.then_inc(self.sem, 1)
        self.n = self.n + 1
        self.steps += 1
        if passed is None:
            self.eng.wait_ge(self.sem, self.n)
        else:
            wait_alone(self.eng, self.sem, self.n, passed)

    @contextmanager
    def loop(self, count, steps, first=0):
        start, seen = self.n, self.steps
        with self.eng.Fori(first, first + count) as i:
            self.n = start + (i - first) * steps
            yield i
        self.n = start + count * steps
        assert self.steps - seen == steps, (self.steps - seen, steps)
        self.steps = seen + count * steps


def later(t):
    return not (isinstance(t, int) and t < 2)


def over_tiles(body, loop, tiles):
    total = [0, 0]
    ends = [first for first, _ in RUNS[1:]] + [tiles]
    for (first, slots), end in zip(RUNS, ends):
        if end - first <= 2:
            for t in range(first, end):
                total[t % 2] += slots
                body(t, t % 2, t // 2, slots, total[t % 2])
            continue
        with loop((end - first) // 2, first // 2) as half:
            for b in range(2):
                body(2 * half + b, b, half, slots, (half - (first // 2 - 1)) * slots + total[b])
        for b in range(2):
            total[b] += (end - first) // 2 * slots


def slots_of(tiles):
    total = [0, 0]
    ends = [first for first, _ in RUNS[1:]] + [tiles]
    for (first, slots), end in zip(RUNS, ends):
        for t in range(first, end):
            total[t % 2] += slots
    return total


def build(nc, x, adj, Wq, Wk, Wv, W1, b1, W2, b2, W2h, b2h, W3, a3, out):
    N, D = x.shape
    T = N // P
    CH = N // 512
    Q = N // 1024
    x_rows = x.rearrange("(t p) d -> p t d", p=P)
    out_rows = out.rearrange("(t p) d -> p t d", p=P)

    with ExitStack() as ctx:
        def sb(name, shape, dt=F32):
            return ctx.enter_context(nc.sbuf_tensor(name, shape, dt))

        def pb(name, shape):
            return ctx.enter_context(nc.psum_tensor(name, shape, F32))

        def sem(name):
            return ctx.enter_context(nc.semaphore(name))

        wq, wk, wv, w1, w2, w3 = (sb(n, [P, D]) for n in ("wq", "wk", "wv", "w1", "w2", "w3"))
        wT = sb("wT", [P, 4, D])
        a_cols = sb("a_cols", [P, 2])
        b1_col = sb("b1_col", [P, 1])
        b2_rows = sb("b2_rows", [P, D])
        head_cols = sb("head_cols", [P, HEADS])
        head_bias = sb("head_bias", [P, HEADS])
        w_qk = sb("w_qk", [P, D])
        w_v1 = sb("w_v1", [P, D])
        w_a = sb("w_a", [P, 2])
        w_a2 = sb("w_a2", [P, P])
        ones = sb("ones", [P, P])
        ident = sb("ident", [P, P])
        ident_b = sb("ident_b", [P, P], BF16)

        rows = sb("rows", [P, T, W_X + D], U32)
        xs = rows[:, :, W_X:].bitcast(F32)
        hs = sb("hs", [P, T, D])
        hT = sb("hT", [P, N])
        stats = sb("stats", [P, T, 6])
        mean, gap, var = sb("mean", [P, T]), sb("gap", [P, T]), sb("var", [P, T])
        std, rstd, shift = sb("std", [P, T]), sb("rstd", [P, T]), sb("shift", [P, T])
        h_tile = sb("h_tile", [P, D])
        u_tile = sb("u_tile", [P, D])
        uT_tile = sb("uT_tile", [P, P])
        hid_tile = sb("hid_tile", [P, P])
        sum_tile = sb("sum_tile", [P, D])
        max_col = sb("max_col", [P, 1])
        negmax = sb("negmax", [P, 1])
        denom = sb("denom", [P, 1])
        rdenom = sb("rdenom", [P, 1])

        adj_bufs = sb("adj_bufs", [P, 3, N], I32)
        work = sb("work", [P, 3, N])

        adj_tile = adj_bufs[:, 0, :]
        scores = work[:, 0, :]
        probs = work[:, 1, :]
        mask_b = work[:, 2, 0:N // 2].bitcast(BF16)
        chunk_a = sb("chunk_a", [P, 1024])
        chunk_b = sb("chunk_b", [P, 512])
        pT = sb("pT", [P, 2, 512])
        queries = sb("queries", [P, HEADS, P])

        G8 = N // GROUP * TOP
        iota_n = work[:, 2, :]
        cand = sb("cand", [P, 2, 2, G8])
        top24 = sb("top24", [P, 2, SLOTS])
        keys = sb("keys", [P, T, SLOTS])
        group_full = sb("group_full", [P, T])
        square_sums = sb("square_sums", [P, T])
        weight_squares = sb("weight_squares", [P, 8])
        totals = sb("totals", [P, 8])
        square_out = sb("square_out", [P, N], BF16)
        minus_half = sb("minus_half", [P, 1])
        bad_cols = sb("bad_cols", [P, 16])
        bad_col = sb("bad_col", [P, 1])
        bad_flag = sb("bad_flag", [P, 1], I32)
        small = sb("small", [P, 4])

        C = SLOTS + 1
        CT = C * T
        degree = sb("degree", [P, T])
        class_iota = work[:, 0, 0:CT]
        onehot = work[:, 0, CT:2 * CT]
        run_sum = [work[:, 0, 2 * CT:3 * CT], work[:, 0, 3 * CT:4 * CT]]
        class_total = work[:, 0, 4 * CT:5 * CT]
        filled = work[:, 1, 0:T * SLOTS]
        onehot_b = sb("onehot_b", [P, CT], BF16)
        before_b = sb("before_b", [P, P], BF16)
        ones_b = sb("ones_b", [P, P], BF16)
        place = sb("place", [P, T])
        place_u = sb("place_u", [P, T], U32)

        W3R = D + 1
        gathered = [work[:, 0, :], work[:, 1, :]]
        weighted = work[:, 2, :]
        q_rows = adj_bufs[:, 2, :].bitcast(F32).rearrange("p (t d) -> p t d", d=D)
        zero_scores = adj_bufs[:, 0, :].bitcast(F32)
        zero_probs = adj_bufs[:, 1, :].bitcast(F32)
        pad_bias = keys
        no_nbr = sb("no_nbr", [P, T])
        f1_rows = sb("f1_rows", [P, T])
        zero_row = sb("zero_row", [P, D])
        w0_rows = sb("w0_rows", [P, D])
        table_pad = sb("table_pad", [1, W3R])
        eps_col = sb("eps_col", [P, 1])
        slots_s = sb("slots_s", [P, 2, SLOTS], U32)
        node_s = sb("node_s", [P, 2, 1], U32)
        score_s = sb("score_s", [P, 2, SLOTS])
        prob_s = sb("prob_s", [P, 2, SLOTS])
        negmax_s = sb("negmax_s", [P, 2, 1])
        denom_s = sb("denom_s", [P, 2, 1])
        rdenom_s = sb("rdenom_s", [P, 2, 1])
        u_s = sb("u_s", [P, 2, D])
        uT_s = sb("uT_s", [P, 2, P])
        hid_s = sb("hid_s", [P, 2, P])
        sum_s = sb("sum_s", [P, 2, D])
        bn_s = sb("bn_s", [P, 2, 6])
        mv_s = sb("mv_s", [P, 2, 2])
        std_s = sb("std_s", [P, 2, 1])
        rstd_s = sb("rstd_s", [P, 2, 1])
        shift_s = sb("shift_s", [P, 2, 1])
        h_s = sb("h_s", [P, 2, W3R])
        hT_s = sb("hT_s", [P, 2, P])
        widths = [D, D, D, W3R]
        tables = [nc.dram_tensor(f"table{layer}", (N + 1, widths[layer]), F32).ap() for layer in range(LAYERS)]
        sorted_rows = nc.dram_tensor("sorted_rows", (N, W_X + D), U32).ap()
        f1_col = sb("f1_col", [P, 1])
        quarter_max = sb("quarter_max", [P, Q])
        maxT = sb("maxT", [P, P])

        ps_big = pb("ps_big", [P, 4, 512])
        ps_t = pb("ps_t", [P, 512])
        ps_acc = pb("ps_acc", [P, 512])
        ps_e = pb("ps_e", [P, 512])
        ps_f = pb("ps_f", [P, 512])
        ps_uT, ps_hid, ps_delta, ps_hT = (ps_big[:, i, :] for i in range(4))

        x_in = sem("x_in")
        weights_in = sem("weights_in")
        ident_zeroed = sem("ident_zeroed")
        ident_ready = sem("ident_ready")
        wT_ready = sem("wT_ready")
        wT_copied = sem("wT_copied")
        products_ready = sem("products_ready")
        products_copied = sem("products_copied")
        dve_step = sem("dve_step")
        out_done = sem("out_done")

        def sems(name, *layers):
            return {layer: sem(f"{name}{layer}") for layer in layers or range(LAYERS)}

        norm_ready = sems("norm_ready")
        h_ready = sems("h_ready")
        var_ready = sems("var_ready")
        std_ready = sems("std_ready")
        hT_ready = sems("hT_ready")
        h_stored = sems("h_stored")
        adj_in = sem("adj_in")
        adj_free = sem("adj_free")
        u_ready = sems("u_ready", 1, 2, 3)
        uT_ready = sems("uT_ready", 1, 3)
        uT_copied = sems("uT_copied", 1, 3)
        hid_ready = sems("hid_ready", 1)
        hid_copied = sems("hid_copied", 1)
        delta_ready = sems("delta_ready", 1, 3)
        elu_in = sems("elu_in", 3)
        elu_exp = sems("elu_exp", 3)
        x_updated = sem("x_updated")
        mask_ready = sem("mask_ready")
        quarters_ready = sem("quarters_ready")
        quarters_used = sem("quarters_used")
        maxT_ready = sem("maxT_ready")
        max_ready = sem("max_ready")
        row_max_taken = sem("row_max_taken")
        u_copied = sems("u_copied", 1, 2, 3)
        lhs_made = sems("lhs_made", 3)
        lhs_product = sems("lhs_product", 1, 3)
        lhs_ready = sems("lhs_ready", 1, 2, 3)
        banks_ready = sems("banks_ready", 1, 2, 3)
        banks_used = sems("banks_used", 1, 2, 3)
        rowmax_ready = sems("rowmax_ready", 1, 2, 3)
        probs_ready = sems("probs_ready", 1, 2, 3)
        pT_ready = sems("pT_ready", 1, 2, 3)
        pT_copied = sems("pT_copied", 1, 2, 3)
        pv_done = sems("pv_done", 1, 2, 3)

        consts_ready = sem("consts_ready")
        pads_in = sem("pads_in")
        scan_in = [sem("scan_in_even"), sem("scan_in_odd")]
        keys_made = sem("keys_made")
        squares_done = sem("squares_done")
        weights_squared = sem("weights_squared")
        onehot_ready = sem("onehot_ready")
        prefix_ready = sem("prefix_ready")
        places_ready = sem("places_ready")
        rows_scattered = sem("rows_scattered")
        rows_sorted = sem("rows_sorted")
        bad_ready = sem("bad_ready")
        bad_summed = sem("bad_summed")
        flag_ready = sem("flag_ready")
        table0_in = sem("table0_in")
        slots_in = [sem(f"slots_in{b}") for b in range(2)]
        gather_in = [sem(f"gather_in{b}") for b in range(2)]
        gather_used = sem("gather_used")
        bn_ready = sems("bn_ready", 0, 1, 2)
        row_std_ready = sems("row_std_ready", 0, 1, 2)
        row_norm_ready = sems("row_norm_ready", 0, 1, 2)
        row_ready = sems("row_ready", 0, 1, 2)
        scattered = [sem(f"scattered{b}") for b in range(2)]
        rowT_ready = sems("rowT_ready", 0, 1, 2)
        rowT_copied = sems("rowT_copied", 0, 2)
        row_q_ready = sems("row_q_ready", 0, 2)
        row_used = sems("row_used", 0, 1)
        sparse_scores = sems("sparse_scores", 1, 2, 3)
        sparse_probs = sems("sparse_probs", 1, 2, 3)
        zero_ready = sem("zero_ready")
        q_copied = sems("q_copied", 0, 2)
        x_again = sem("x_again")
        table0_ready = sem("table0_ready")
        pad_row_ready = sem("pad_row_ready")
        node_zeroed = sem("node_zeroed")
        node_ready = sem("node_ready")
        iota_ready = sem("iota_ready")
        classes_ready = sem("classes_ready")
        scan_done = sem("scan_done")
        dve_passed = sem("dve_passed")
        pool_passed = sem("pool_passed")
        final_ready = sems("final_ready", 3)

        block = ctx.enter_context(nc.Block())
        WEIGHTS = 16 * 13
        heads = [0, 1, HEADS, 1]

        @block.sync
        def _(sp):
            sp.dma_start(xs, x_rows).then_inc(x_in, 16)
            for dst, src in ((wq, Wq), (wk, Wk), (wv, Wv), (w1, W1), (w2, W2), (w3, W3)):
                sp.dma_start(dst[:, :], src).then_inc(weights_in, 16)
            for c in range(2):
                sp.dma_start(a_cols[:, c:c + 1], a3[c * D:(c + 1) * D, :]).then_inc(weights_in, 16)
            sp.dma_start(b1_col[:, :], b1.rearrange("(p o) -> p o", o=1)).then_inc(weights_in, 16)
            sp.dma_start(b2_rows[:, :], b2.partition_broadcast(P)).then_inc(weights_in, 16)
            sp.dma_start(head_cols[:, :], W2h.rearrange("k d -> d k"), allow_slow_non_contiguous=True).then_inc(weights_in, 16)
            sp.dma_start(head_bias[:, :], b2h.partition_broadcast(P)).then_inc(weights_in, 16)
            sp.dma_start(w0_rows[:, :], W2h[0, :].partition_broadcast(P)).then_inc(weights_in, 16)
            for b in range(2):
                sp.dma_start(adj_bufs[:, b, :], adj[b * P:(b + 1) * P, :]).then_inc(scan_in[b], 16)
            with sp.Fori(1, T // 2) as half:
                for b in range(2):
                    sp.wait_ge(keys_made, 2 * half + b - 1)
                    sp.wait_ge(squares_done, 2 * half + b - 1)
                    sp.dma_start(adj_bufs[:, b, :], adj[bass.ds((2 * half + b) * P, P), :]).then_inc(scan_in[b], 16)
            sp.wait_ge(table0_ready, T)
            sp.dma_start(tables[0][0:N, :].rearrange("(t p) d -> p t d", p=P), hs[:, :, :]).then_inc(table0_in, 16)
            sp.wait_ge(pad_row_ready, 1)
            for layer in range(LAYERS):
                sp.dma_start(tables[layer][N:N + 1, :], table_pad[:, 0:widths[layer]]).then_inc(pads_in, 16)
            sp.wait_ge(rows_scattered, 16 * T)
            sp.dma_start(rows[:, :, :], sorted_rows.rearrange("(t p) w -> p t w", p=P)).then_inc(rows_sorted, 16)

            sp.wait_ge(table0_in, 16)
            sp.wait_ge(pads_in, 16 * LAYERS)

            def sparse():
                all_slots = slots_of(T)
                for layer in range(LAYERS):
                    def body(t, b, half, slots, done):
                        if not later(t):
                            if layer:
                                sp.wait_ge(gather_in[b], 16 * layer * all_slots[b])
                        else:
                            sp.wait_ge(gather_in[b], 16 * (done - slots + layer * all_slots[b]))
                        sp.dma_start(slots_s[:, b, :], rows[:, bass.ds(t, 1), 0:SLOTS].rearrange("p o k -> p (o k)"))\
                            .then_inc(slots_in[b], 16)

                    over_tiles(body, lambda count, first: sp.Fori(first, first + count), T)
                for b in range(2):
                    sp.wait_ge(scattered[b], 16 * LAYERS * (T // 2))

            def dense():
                sp.dma_start(xs, x_rows).then_inc(x_again, 16)
                for layer in range(LAYERS):
                    if layer:
                        sp.wait_ge(adj_free, layer * T)
                    sp.dma_start(adj_tile, adj[0:P, :]).then_inc(adj_in, 16)
                    with sp.Fori(1, T) as t:
                        sp.wait_ge(adj_free, layer * T + t)
                        sp.dma_start(adj_tile, adj[bass.ds(t * P, P), :]).then_inc(adj_in, 16)
                sp.wait_ge(x_updated, LAYERS * T)
                sp.dma_start(out_rows, xs).then_inc(out_done, 16)
                sp.wait_ge(out_done, 16)

            sp.wait_ge(flag_ready, 1)
            bad = sp.value_load(bad_flag[0:1, 0:1])
            with sp.If(bad > 0):
                dense()
            with sp.Else():
                sparse()

        @block.gpsimd
        def _(pool):
            pool.memset(ident[:, :], 0.0).then_inc(ident_zeroed, 1)
            pool.memset(ident_b[:, :], 0.0).then_inc(ident_zeroed, 1)
            pool.memset(ones_b[:, :], 1.0).then_inc(ident_zeroed, 1)
            pool.memset(ones[:, :], 1.0).then_inc(ident_ready, 1)
            pool.wait_ge(ident_zeroed, 3)
            for m in (ident, ident_b):
                pool.affine_select(out=m[:, :], in_=m[:, :], compare_op=ALU.not_equal, fill=1.0, base=0,
                                   pattern=[[-1, P]], channel_multiplier=1).then_inc(ident_ready, 1)
            pool.memset(weight_squares[:, :], 0.0).then_inc(consts_ready, 1)
            pool.memset(minus_half[:, :], -0.5).then_inc(consts_ready, 1)
            pool.memset(eps_col[:, :], LN_EPS).then_inc(consts_ready, 1)
            pool.memset(bad_cols[:, :], 0.0).then_inc(consts_ready, 1)
            pool.affine_select(out=before_b[:, :], in_=ones_b[:, :], compare_op=ALU.is_gt, fill=0.0, base=0,
                               pattern=[[1, P]], channel_multiplier=-1).then_inc(consts_ready, 1)
            pool.iota(iota_n, [[1, N]], base=1, channel_multiplier=0,
                      allow_small_or_imprecise_dtypes=True).then_inc(iota_ready, 1)
            pool.memset(table_pad[:, :], 0.0).then_inc(pad_row_ready, 1)
            pool.memset(rows[:, :, SLOTS:W_X], 0).then_inc(node_zeroed, 1)
            pool.wait_ge(node_zeroed, 1)
            pool.iota(rows[:, :, W_NODE:W_NODE + 1], [[P, T], [0, 1]], base=0, channel_multiplier=1).then_inc(node_ready, 1)

            pool.wait_ge(scan_done, 1)
            pool.iota(class_iota.rearrange("p (c t) -> p c t", t=T), [[-1, C], [0, T]], base=SLOTS,
                      channel_multiplier=0, allow_small_or_imprecise_dtypes=True).then_inc(classes_ready, 1)
            pool.wait_ge(node_ready, 1)
            pool.wait_ge(places_ready, 1)
            for t in range(T):
                pool.indirect_dma_start(sorted_rows, bass.IndirectOffsetOnAxis(ap=place_u[:, t:t + 1], axis=0),
                                        rows[:, t, :], None).then_inc(rows_scattered, 16)

            def sparse():
                for layer in range(LAYERS):
                    width = widths[layer]
                    pool.wait_ge(pads_in, 16 * LAYERS)
                    if layer == 0:
                        pool.wait_ge(table0_in, 16)
                    else:
                        for b in range(2):
                            pool.wait_ge(scattered[b], 16 * layer * (T // 2))
                    ready = {0: row_ready, 1: row_ready, 2: q_copied, 3: final_ready}[layer][layer]

                    def scatter(t, b):
                        wait_alone(pool, ready, t + 1, pool_passed)
                        last = layer == LAYERS - 1
                        dst, columns = (out, D) if last else (tables[layer + 1], widths[layer + 1])
                        pool.indirect_dma_start(dst, bass.IndirectOffsetOnAxis(ap=node_s[:, b, :], axis=0),
                                                h_s[:, b, 0:columns], None).then_inc(scattered[b], 16)

                    def body(t, b, half, slots, done):
                        if later(t):
                            pool.wait_ge(gather_used, t - 1 + layer * T)
                        wait_alone(pool, slots_in[b], 16 * (half + 1 + layer * (T // 2)), pool_passed)
                        for k in range(slots):
                            pool.indirect_dma_start(gathered[b][:, k * width:(k + 1) * width], None, tables[layer],
                                                    bass.IndirectOffsetOnAxis(ap=slots_s[:, b, k:k + 1], axis=0))\
                                .then_inc(gather_in[b], 16)
                        if later(t):
                            scatter(t - 2, b)

                    over_tiles(body, lambda count, first: pool.Fori(first, first + count), T)
                    scatter(T - 2, 0)
                    scatter(T - 1, 1)

            pool.wait_ge(flag_ready, 1)
            bad = pool.value_load(bad_flag[0:1, 0:1])
            with pool.If(bad > 0):
                pool.wait_ge(x_again, 16)
            with pool.Else():
                sparse()

        @block.tensor
        def _(pe):
            pe.wait_ge(ident_ready, 3)
            pe.wait_ge(weights_in, WEIGHTS)
            for i, w in enumerate((wq, wk, wv, w3)):
                mm = pe.transpose(ps_t[:, i * P:(i + 1) * P], w[:, :], ident[:, :])
            mm.then_inc(wT_ready, 1)
            pe.wait_ge(wT_copied, 1)
            pe.matmul(ps_e[:, 0:D], wT[:, 0, :], wT[:, 1, :], start=True, stop=True)
            pe.matmul(ps_acc[:, 0:D], wT[:, 2, :], w1[:, :], start=True, stop=True)
            pe.matmul(ps_f[:, 0:2], wT[:, 3, :], a_cols[:, :], start=True, stop=True)
            pe.wait_ge(weights_squared, 6)
            pe.matmul(ps_f[:, 64:72], ones[:, :], weight_squares[:, :], start=True, stop=True).then_inc(products_ready, 1)
            pe.wait_ge(products_copied, 1)

            pe.wait_ge(consts_ready, 5)
            pe.wait_ge(onehot_ready, 1)
            h2 = CT // 2
            for i in range(2):
                pe.matmul(ps_big[:, i, 0:h2], before_b[:, :], onehot_b[:, i * h2:(i + 1) * h2], start=True, stop=True)
            for i in range(2):
                mm = pe.matmul(ps_big[:, 2 + i, 0:h2], ones_b[:, :], onehot_b[:, i * h2:(i + 1) * h2],
                               start=True, stop=True)
            mm.then_inc(prefix_ready, 1)
            pe.wait_ge(bad_ready, 1)
            pe.matmul(ps_f[:, 0:1], ones[:, :], bad_col[:, :], start=True, stop=True).then_inc(bad_summed, 1)

            def transpose_rows(layer):
                with pe.Fori(0, T) as t:
                    pe.wait_ge(h_ready[layer], t + 1)
                    pe.transpose(ps_t[:, 0:P], h_tile[:, :], ident[:, :]).then_inc(hT_ready[layer], 1)
                pe.wait_ge(h_stored[layer], T + 1)

            def finish(layer, n):
                if layer == 2:
                    return
                pe.wait_ge(u_ready[layer], n + 1)
                pe.transpose(ps_e[:, 0:P], u_tile[:, :], ident[:, :]).then_inc(uT_ready[layer], 1)
                pe.wait_ge(uT_copied[layer], n + 1)
                if layer == 1:
                    pe.matmul(ps_f[:, 0:P], w_v1[:, :], uT_tile[:, :], start=True, stop=True).then_inc(hid_ready[layer], 1)
                    pe.wait_ge(hid_copied[layer], n + 1)
                    pe.matmul(ps_e[:, 0:D], hid_tile[:, :], w2[:, :], start=True, stop=True).then_inc(delta_ready[layer], 1)
                else:
                    pe.matmul(ps_f[:, 0:D], uT_tile[:, :], w3[:, :], start=True, stop=True).then_inc(delta_ready[layer], 1)

            def attend(layer, t, lhs, probs):
                banks = CH * heads[layer]
                pe.wait_ge(lhs_ready[layer], t + 1)
                for i in range(banks):
                    c, k = divmod(i, heads[layer])
                    pe.wait_ge(banks_used[layer], t * banks + i + 1)
                    pe.matmul(ps_big[:, i % 2, :], lhs(k), hT[:, c * 512:(c + 1) * 512],
                              start=True, stop=True).then_inc(banks_ready[layer], 1)
                pe.wait_ge(probs_ready[layer], t + 1)
                for c in range(CH + 1):
                    if c < CH:
                        if c >= 2:
                            pe.wait_ge(pT_copied[layer], t * CH + c - 1)
                        for b in range(4):
                            j = c * 4 + b
                            mm = pe.transpose(ps_big[:, 2 + c % 2, b * P:(b + 1) * P],
                                              probs[:, j * P:(j + 1) * P], ident[:, :])
                        mm.then_inc(pT_ready[layer], 1)
                    if c:
                        pe.wait_ge(pT_copied[layer], t * CH + c)
                        for b in range(4):
                            j = (c - 1) * 4 + b
                            mm = pe.matmul(ps_acc[:, 0:D], pT[:, (c - 1) % 2, b * P:(b + 1) * P], hs[:, j, :],
                                           start=(j == 0), stop=(j == T - 1))
                        mm.then_inc(pv_done[layer], 1)

            def dense():
                transpose_rows(0)
                with pe.Fori(0, T) as t:
                    with pe.Fori(0, P) as r:
                        pe.wait_ge(mask_ready, t + 1)
                        for q in range(Q):
                            pe.wait_ge(quarters_used, (t * P + r) * Q + q + 1)
                            for half in range(2):
                                c = 2 * q + half
                                mm = pe.matmul(ps_big[:, 2 * (q % 2) + half, :],
                                               ident_b[:, bass.ds(r, 1)].to_broadcast([P, P]),
                                               mask_b[:, c * 512:(c + 1) * 512], start=True, stop=True)
                            mm.then_inc(quarters_ready, 1)
                    pe.wait_ge(maxT_ready, t + 1)
                    pe.transpose(ps_t[:, 0:P], maxT[:, :], ident[:, :]).then_inc(max_ready, 1)

                for layer in range(1, LAYERS):
                    transpose_rows(layer)
                    with pe.Fori(0, T) as t:
                        if layer == 1:
                            pe.matmul(ps_t[:, 0:P], w_qk[:, :], hT[:, bass.ds(t * P, P)], start=True,
                                      stop=True).then_inc(lhs_product[layer], 1)
                        if layer == 3:
                            pe.wait_ge(lhs_made[layer], t + 1)
                            pe.matmul(ps_t[:, 0:1], queries[:, 0, :], w_a[:, 0:1], start=True,
                                      stop=True).then_inc(lhs_product[layer], 1)
                        attend(layer, t, lambda k: w_a2[:, :] if layer == 3 else queries[:, k, :], probs)
                        finish(layer, t)

            def sparse():
                for layer in range(LAYERS):
                    following = layer + 1
                    if layer == 1:
                        pe.wait_ge(row_used[0], T)
                        pe.wait_ge(q_copied[0], T)
                        pe.matmul(ps_t[:, 0:P], w_qk[:, :], hT[:, N - P:N], start=True, stop=True)\
                            .then_inc(lhs_product[layer], 1)
                        attend(layer, 0, lambda k: queries[:, 0, :], zero_probs)
                        pe.wait_ge(zero_ready, 1)

                    def finish_first(t, b):
                        if layer in (1, 3):
                            pe.wait_ge(u_ready[layer], t + 1)
                            pe.transpose(ps_uT[:, 0:P], u_s[:, b, :], ident[:, :]).then_inc(uT_ready[layer], 1)
                            pe.wait_ge(uT_copied[layer], t + 1)
                            if layer == 1:
                                pe.matmul(ps_hid[:, 0:P], w_v1[:, :], uT_s[:, b, :], start=True,
                                          stop=True).then_inc(hid_ready[layer], 1)
                            else:
                                pe.matmul(ps_delta[:, 0:P], uT_s[:, b, :], w3[:, :], start=True,
                                          stop=True).then_inc(delta_ready[layer], 1)

                    def finish_last(t, b):
                        if layer == 1:
                            pe.wait_ge(hid_copied[layer], t + 1)
                            pe.matmul(ps_delta[:, 0:D], hid_s[:, b, :], w2[:, :], start=True,
                                      stop=True).then_inc(delta_ready[layer], 1)

                    def prepare(t, b):
                        if following == LAYERS:
                            return
                        pe.wait_ge(row_ready[layer], t + 1)
                        if following >= 2:
                            mm = pe.matmul(ps_acc[:, 0:D], ones[:, :], h_s[:, b, 0:D],
                                           start=isinstance(t, int) and t == 0, stop=isinstance(t, int) and t == T - 1)
                        if following != 2:
                            if following == 1 and not (isinstance(t, int) and t == 0):
                                pe.wait_ge(row_used[layer], t)
                            mm = pe.transpose(ps_hT[:, 0:P], h_s[:, b, 0:D], ident[:, :])
                        mm.then_inc(rowT_ready[layer], 1)
                        if following != 2:
                            pe.wait_ge(rowT_copied[layer], t + 1)
                            if not (isinstance(t, int) and t == 0):
                                pe.wait_ge(q_copied[layer], t)
                            columns, w = (D, w_qk) if following == 1 else (2, w_a)
                            pe.matmul(ps_t[:, 0:columns], hT_s[:, b, :], w[:, 0:columns], start=True,
                                      stop=True).then_inc(row_q_ready[layer], 1)

                    def body(t, b, half, slots, done):
                        finish_first(t, b)
                        if not (isinstance(t, int) and t == 0):
                            prepare(t - 1, 1 - b)
                        finish_last(t, b)

                    over_tiles(body, lambda count, first: pe.Fori(first, first + count), T)
                    prepare(T - 1, 1)

            pe.wait_ge(flag_ready, 1)
            bad = pe.value_load(bad_flag[0:1, 0:1])
            with pe.If(bad > 0):
                dense()
            with pe.Else():
                sparse()

        @block.scalar
        def _(act):
            def row_tile(a, t):
                return a[:, bass.ds(t, 1), :].rearrange("p o d -> p (o d)")

            def row_std(layer):
                act.wait_ge(var_ready[layer], 1)
                act.activation(std[:, :], var[:, :], ACT.Sqrt).then_inc(std_ready[layer], 1)

            def normalise(layer):
                if layer:
                    row_std(layer)
                    act.wait_ge(norm_ready[layer], 1)
                with act.Fori(0, T) as t:
                    act.wait_ge(h_stored[layer], t + 1)
                    if layer:
                        act.activation(h_tile[:, :], row_tile(xs, t), ACT.Relu, bias=shift[:, bass.ds(t, 1)],
                                       scale=rstd[:, bass.ds(t, 1)]).then_inc(h_ready[layer], 1)
                    else:
                        act.activation(h_tile[:, :], row_tile(hs, t), ACT.Copy).then_inc(h_ready[layer], 1)

            def finish(layer, n):
                if layer == 1:
                    act.wait_ge(hid_ready[layer], n + 1)
                    act.activation(hid_tile[:, :], ps_f[:, 0:P], ACT.Relu, bias=b1_col[:, :]).then_inc(hid_copied[layer], 1)
                if layer == 3:
                    act.wait_ge(elu_in[layer], n + 1)
                    act.activation(hid_tile[:, :], sum_tile[:, :], ACT.Exp).then_inc(elu_exp[layer], 1)

            def attend(layer, t, scores, probs):
                act.wait_ge(rowmax_ready[layer], t + 1)
                act.activation(probs, scores, ACT.Exp, bias=negmax[:, :],
                               accum_out=denom[:, :]).then_inc(probs_ready[layer], 1)
                for c in range(CH):
                    act.wait_ge(pT_ready[layer], t * CH + c + 1)
                    if c >= 2:
                        act.wait_ge(pv_done[layer], t * CH + c - 1)
                    act.activation(pT[:, c % 2, :], ps_big[:, 2 + c % 2, :], ACT.Copy).then_inc(pT_copied[layer], 1)

            act.wait_ge(weights_in, WEIGHTS)
            act.wait_ge(consts_ready, 5)
            for i, (w, columns) in enumerate(((wq, D), (wk, D), (w3, D), (a_cols, 2), (head_cols, HEADS), (head_bias, HEADS))):
                act.activation(hT[:, i * D:i * D + columns], w[:, 0:columns], ACT.Square,
                               accum_out=weight_squares[:, i:i + 1]).then_inc(weights_squared, 1)
            row_std(0)
            act.wait_ge(norm_ready[0], 1)
            with act.Fori(0, T) as t:
                act.activation(row_tile(hs, t), row_tile(xs, t), ACT.Relu, bias=shift[:, bass.ds(t, 1)],
                               scale=rstd[:, bass.ds(t, 1)]).then_inc(table0_ready, 1)
            with act.Fori(0, T // 2) as half:
                for b in range(2):
                    act.wait_ge(scan_in[b], 16 * (half + 1))
                    act.activation(square_out[:, :], adj_bufs[:, b, :], ACT.Square, bias=minus_half[:, :],
                                   accum_out=square_sums[:, bass.ds(2 * half + b, 1)]).then_inc(squares_done, 1)
                    act.wait_ge(squares_done, 2 * half + b + 1)

            def dense():
                normalise(0)
                for layer in range(1, LAYERS):
                    normalise(layer)
                    with act.Fori(0, T) as t:
                        attend(layer, t, scores, probs)
                        finish(layer, t)

            def sparse():
                for layer in range(LAYERS):
                    following = layer + 1
                    if layer == 1:
                        attend(layer, 0, zero_scores, zero_probs)

                    def row_h(t, b):
                        if following == LAYERS:
                            return
                        act.wait_ge(row_norm_ready[layer], t + 1)
                        if later(t):
                            act.wait_ge(rowT_ready[layer], t - 1)
                            if following != 3:
                                act.wait_ge(row_used[layer], t - 1)
                        act.activation(h_s[:, b, 0:D], row_tile(xs, t), ACT.Relu, bias=shift_s[:, b, :],
                                       scale=rstd_s[:, b, :]).then_inc(row_ready[layer], 1)
                        if following != 2:
                            act.wait_ge(rowT_ready[layer], t + 1)
                            act.activation(hT_s[:, b, :], ps_hT[:, 0:P], ACT.Copy).then_inc(rowT_copied[layer], 1)
                            act.wait_ge(row_q_ready[layer], t + 1)
                            if following == 1:
                                act.activation(row_tile(q_rows, t), ps_t[:, 0:P], ACT.Copy)\
                                    .then_inc(q_copied[layer], 1)
                            else:
                                act.activation(f1_rows[:, bass.ds(t, 1)], ps_t[:, 0:1], ACT.Copy)
                                act.activation(h_s[:, b, D:D + 1], ps_t[:, 1:2], ACT.Copy)\
                                    .then_inc(q_copied[layer], 1)

                    def row_deviation(t, b):
                        if following == LAYERS:
                            return
                        act.wait_ge(bn_ready[layer], t + 1)
                        act.activation(std_s[:, b, :], mv_s[:, b, 1:2], ACT.Sqrt,
                                       bias=eps_col[:, :]).then_inc(row_std_ready[layer], 1)

                    def body(t, b, half, slots, done):
                        first = isinstance(t, int) and t == 0
                        if layer:
                            act.wait_ge(sparse_scores[layer], t + 1)
                            act.activation(prob_s[:, b, 0:slots], score_s[:, b, 0:slots], ACT.Exp, bias=negmax_s[:, b, :],
                                           accum_out=denom_s[:, b, :]).then_inc(sparse_probs[layer], 1)
                        if not first:
                            row_deviation(t - 1, 1 - b)
                        if layer in (1, 3):
                            act.wait_ge(uT_ready[layer], t + 1)
                            act.activation(uT_s[:, b, :], ps_uT[:, 0:P], ACT.Copy).then_inc(uT_copied[layer], 1)
                        if not first:
                            row_h(t - 1, 1 - b)
                        if layer == 1:
                            act.wait_ge(hid_ready[layer], t + 1)
                            act.activation(hid_s[:, b, :], ps_hid[:, 0:P], ACT.Relu,
                                           bias=b1_col[:, :]).then_inc(hid_copied[layer], 1)
                        if layer == 3:
                            act.wait_ge(delta_ready[layer], t + 1)
                            act.activation(hid_s[:, b, :], ps_delta[:, 0:P], ACT.Exp).then_inc(elu_exp[layer], 1)

                    over_tiles(body, lambda count, first: act.Fori(first, first + count), T)
                    row_deviation(T - 1, 1)
                    row_h(T - 1, 1)

            act.wait_ge(flag_ready, 1)
            bad = act.value_load(bad_flag[0:1, 0:1])
            with act.If(bad > 0):
                dense()
            with act.Else():
                sparse()

        @block.vector
        def _(dve):
            step = Chain(dve, dve_step)

            def row_tile(a, t):
                return a[:, bass.ds(t, 1), :].rearrange("p o d -> p (o d)")

            dve.wait_ge(ident_ready, 3)
            dve.wait_ge(wT_ready, 1)
            dve.tensor_copy(wT[:, :, :].rearrange("p a d -> p (a d)"), ps_t[:, :]).then_inc(wT_copied, 1)
            dve.wait_ge(products_ready, 1)
            step(dve.tensor_copy(w_qk[:, :], ps_e[:, 0:D]))
            step(dve.tensor_copy(w_v1[:, :], ps_acc[:, 0:D]))
            step(dve.tensor_copy(w_a[:, :], ps_f[:, 0:2]))
            dve.tensor_scalar(w_a2[:, :], ones[:, :], w_a[:, 1:2], None, ALU.mult).then_inc(products_copied, 1)
            dve.wait_ge(consts_ready, 5)
            step(dve.tensor_copy(totals[:, :], ps_f[:, 64:72]))
            step(dve.tensor_tensor(small[:, 0:1], totals[:, 0:1], totals[:, 1:2], ALU.mult))
            step(dve.tensor_tensor(small[:, 1:2], totals[:, 2:3], totals[:, 3:4], ALU.mult))
            qk_limit = ((NEG_BIG - 200.0) / (2 * D)) ** 2
            for i, (col, limit) in enumerate(((small[:, 0:1], qk_limit), (small[:, 1:2], 1e20),
                                              (totals[:, 4:5], 1e20), (totals[:, 5:6], 1e20))):
                step(dve.tensor_scalar(bad_cols[:, i:i + 1], col, limit, 0.0, ALU.is_lt, ALU.is_equal))
            dve.wait_ge(x_in, 16)

            def layer_stats(layer):
                even_mean, even_m2, odd_mean, odd_m2 = (stats[:, :, i] for i in (1, 2, 4, 5))
                step(dve.tensor_tensor(mean[:, :], even_mean, odd_mean, ALU.add))
                step(dve.tensor_tensor(gap[:, :], even_mean, odd_mean, ALU.subtract))
                step(dve.tensor_tensor(var[:, :], even_m2, odd_m2, ALU.add))
                step(dve.tensor_tensor(gap[:, :], gap[:, :], gap[:, :], ALU.mult))
                step(dve.scalar_tensor_tensor(out=var[:, :], in0=gap[:, :], scalar=D / 4.0, in1=var[:, :],
                                              op0=ALU.mult, op1=ALU.add))
                dve.tensor_scalar(var[:, :], var[:, :], 1.0 / D, LN_EPS, ALU.mult, ALU.add).then_inc(var_ready[layer], 1)
                dve.wait_ge(std_ready[layer], 1)
                step(dve.reciprocal(rstd[:, :], std[:, :]))
                dve.scalar_tensor_tensor(out=shift[:, :], in0=mean[:, :], scalar=-0.5, in1=rstd[:, :],
                                         op0=ALU.mult, op1=ALU.mult).then_inc(norm_ready[layer], 1)

            def row_stats():
                with dve.Fori(0, T) as t:
                    dve.bn_stats(row_tile(stats, t), row_tile(xs, t)).then_inc(dve_step, 1)
                step.n = step.n + T
                dve.wait_ge(dve_step, step.n)

            def normalise(layer):
                if layer:
                    row_stats()
                    layer_stats(layer)
                dve.sem_inc(h_stored[layer], 1)
                with dve.Fori(0, T) as t:
                    dve.wait_ge(h_ready[layer], t + 1)
                    dve.tensor_copy(row_tile(hs, t), h_tile[:, :])
                    dve.wait_ge(hT_ready[layer], t + 1)
                    dve.tensor_copy(hT[:, bass.ds(t * P, P)], ps_t[:, 0:P]).then_inc(h_stored[layer], 1)
                    dve.wait_ge(h_stored[layer], t + 2)

            def finish(layer, n, x_tile):
                if layer == 2:
                    dve.scalar_tensor_tensor(out=x_tile, in0=u_tile[:, :], scalar=rdenom[:, :], in1=x_tile,
                                             op0=ALU.mult, op1=ALU.add).then_inc(x_updated, 1)
                    dve.wait_ge(x_updated, layer * T + n + 1)
                    return
                dve.tensor_scalar(u_tile[:, :], u_tile[:, :], rdenom[:, :], None, ALU.mult).then_inc(u_ready[layer], 1)
                dve.wait_ge(uT_ready[layer], n + 1)
                dve.tensor_copy(uT_tile[:, :], ps_e[:, 0:P]).then_inc(uT_copied[layer], 1)
                dve.wait_ge(delta_ready[layer], n + 1)
                if layer == 1:
                    step(dve.tensor_tensor(sum_tile[:, :], ps_e[:, 0:D], b2_rows[:, :], ALU.add))
                    dve.scalar_tensor_tensor(out=x_tile, in0=sum_tile[:, :], scalar=0.0, in1=x_tile,
                                             op0=ALU.max, op1=ALU.add).then_inc(x_updated, 1)
                else:
                    dve.tensor_scalar(sum_tile[:, :], ps_f[:, 0:D], 0.0, None, ALU.min).then_inc(elu_in[layer], 1)
                    dve.wait_ge(elu_exp[layer], n + 1)
                    step(dve.tensor_scalar(hid_tile[:, :], hid_tile[:, :], -1.0, None, ALU.add))
                    step(dve.scalar_tensor_tensor(out=sum_tile[:, :], in0=ps_f[:, 0:D], scalar=0.0,
                                                  in1=hid_tile[:, :], op0=ALU.max, op1=ALU.add))
                    dve.tensor_tensor(x_tile, x_tile, sum_tile[:, :], ALU.add).then_inc(x_updated, 1)
                dve.wait_ge(x_updated, layer * T + n + 1)

            def find_neighbours():
                dve.wait_ge(iota_ready, 1)
                with step.loop(T // 2, 16) as half:
                    for b in range(2):
                        t = 2 * half + b
                        key = work[:, b, :]
                        dve.wait_ge(scan_in[b], 16 * (half + 1))
                        dve.tensor_tensor(key, adj_bufs[:, b, :], iota_n, ALU.mult).then_inc(keys_made, 1)
                        wait_alone(dve, keys_made, t + 1, dve_passed)
                        for g in range(N // GROUP):
                            top = dve.max(cand[:, b, 0, g * TOP:(g + 1) * TOP], key[:, g * GROUP:(g + 1) * GROUP])
                        step(top)
                        step(dve.tensor_reduce(group_full[:, bass.ds(t, 1)], cand[:, b, 0, TOP - 1:G8:TOP], AX.X, ALU.max),
                             dve_passed)
                        for i in range(SLOTS // TOP):
                            tops = top24[:, b, i * TOP:(i + 1) * TOP]
                            step(dve.max(tops, cand[:, b, i % 2, :]), dve_passed)
                            if i < SLOTS // TOP - 1:
                                step(dve.match_replace(cand[:, b, 1 - i % 2, :], tops, cand[:, b, i % 2, :], 0.0),
                                     dve_passed)
                        step(dve.tensor_copy(row_tile(keys, t), top24[:, b, :]))

            def sort_rows():
                dve.sem_inc(scan_done, 1)
                flat_keys = keys[:, :, :].rearrange("p t k -> p (t k)")
                step(dve.tensor_scalar(filled, flat_keys, 0.0, None, ALU.is_gt))
                step(dve.tensor_reduce(degree[:, :], filled.rearrange("p (t k) -> p t k", k=SLOTS), AX.X, ALU.add))
                step(dve.scalar_tensor_tensor(out=filled, in0=filled, scalar=-(N + 1.0), in1=flat_keys,
                                              op0=ALU.mult, op1=ALU.add))
                step(dve.tensor_scalar(filled, filled, float(N), 0.0, ALU.add, ALU.max))
                dve.wait_ge(node_ready, 1)
                step(dve.tensor_scalar(rows[:, :, 0:SLOTS], filled.rearrange("p (t k) -> p t k", k=SLOTS), float(N),
                                       None, ALU.min))
                dve.wait_ge(classes_ready, 1)
                step(dve.tensor_tensor(onehot.rearrange("p (c t) -> p c t", t=T),
                                       class_iota.rearrange("p (c t) -> p c t", t=T),
                                       degree[:, :].unsqueeze(1).to_broadcast([P, C, T]), ALU.is_equal))
                dve.tensor_copy(onehot_b[:, :], onehot).then_inc(onehot_ready, 1)
                dve.wait_ge(prefix_ready, 1)
                h2 = CT // 2
                step(dve.tensor_copy(class_total.rearrange("p (a b) -> p a b", a=2), ps_big[:, 2:4, 0:h2]))
                src, n, reach = class_total, 0, 1
                while reach < CT:
                    dst = run_sum[n % 2]
                    dve.tensor_copy(dst[:, 0:reach], src[:, 0:reach])
                    step(dve.tensor_tensor(dst[:, reach:], src[:, reach:], src[:, 0:CT - reach], ALU.add))
                    src, n, reach = dst, n + 1, 2 * reach
                step(dve.tensor_tensor(src, src, class_total, ALU.subtract))
                step(dve.tensor_tensor(src.rearrange("p (a b) -> p a b", a=2), src.rearrange("p (a b) -> p a b", a=2),
                                       ps_big[:, 0:2, 0:h2], ALU.add))
                step(dve.tensor_tensor(src, src, onehot, ALU.mult))
                step(dve.tensor_reduce(place[:, :], src.rearrange("p (c t) -> p t c", t=T), AX.X, ALU.add))
                dve.tensor_copy(place_u[:, :], place[:, :]).then_inc(places_ready, 1)
                step(dve.tensor_reduce(bad_cols[:, 4:5], group_full[:, :], AX.X, ALU.max))
                step(dve.tensor_reduce(bad_cols[:, 5:6], keys[:, :, SLOTS - 1], AX.X, ALU.max))
                dve.wait_ge(squares_done, T)
                step(dve.tensor_scalar(square_sums[:, :], square_sums[:, :], N / 4.0, None, ALU.not_equal))
                step(dve.tensor_reduce(bad_cols[:, 6:7], square_sums[:, :], AX.X, ALU.max))
                dve.wait_ge(rows_sorted, 16)
                full = filled.rearrange("p (t k) -> p t k", k=SLOTS)
                step(dve.tensor_scalar(full, rows[:, :, 0:SLOTS], float(N), None, ALU.not_equal))
                step(dve.tensor_scalar(pad_bias[:, :, :], full, -PAD_BIAS, PAD_BIAS, ALU.mult, ALU.add))
                step(dve.tensor_scalar(no_nbr[:, :], full[:, :, 0], -1.0, 1.0, ALU.mult, ALU.add))
                ends = [first for first, _ in RUNS[1:]] + [T]
                for i, ((first, slots), end) in enumerate(zip(RUNS, ends)):
                    step(dve.tensor_reduce(bad_cols[:, 7 + i:8 + i], full[:, first:end, slots], AX.X, ALU.max))
                step(dve.tensor_reduce(bad_cols[:, 7 + len(RUNS):8 + len(RUNS)], no_nbr[:, 0:T - 1], AX.X, ALU.max))
                step(dve.tensor_scalar(bad_cols[:, :], bad_cols[:, :], 0.0, None, ALU.is_gt))
                dve.tensor_reduce(bad_col[:, :], bad_cols[:, :], AX.X, ALU.add).then_inc(bad_ready, 1)
                dve.wait_ge(bad_summed, 1)
                dve.tensor_copy(bad_flag[:, :], ps_f[:, 0:1]).then_inc(flag_ready, 1)

            def dense_scores(layer, t):
                hT_tile = hT[:, bass.ds(t * P, P)]
                banks = CH * heads[layer]
                if layer == 1:
                    dve.wait_ge(lhs_product[layer], t + 1)
                    dve.tensor_copy(queries[:, 0, :], ps_t[:, 0:P]).then_inc(lhs_ready[layer], 1)
                    dve.wait_ge(adj_in, 16 * (layer * T + t + 1))
                    step(dve.tensor_scalar(scores, adj_tile, 0.0, -NEG_BIG, ALU.is_le, ALU.mult))
                    for c in range(CH):
                        part = scores[:, c * 512:(c + 1) * 512]
                        dve.wait_ge(banks_ready[layer], t * banks + c + 1)
                        dve.tensor_tensor(part, part, ps_big[:, c % 2, :], ALU.add).then_inc(banks_used[layer], 1)
                    dve.wait_ge(banks_used[layer], (t + 1) * banks + 2)
                if layer == 2:
                    for k in range(HEADS):
                        ins = dve.tensor_scalar(queries[:, k, :], hT_tile, head_cols[:, k:k + 1], None, ALU.mult)
                    ins.then_inc(lhs_ready[layer], 1)
                    dve.wait_ge(adj_in, 16 * (layer * T + t + 1))
                    step(dve.tensor_scalar(scores, adj_tile, 1.0, None, ALU.is_ge))
                    step(dve.scalar_tensor_tensor(out=scores, in0=adj_tile, scalar=float(HEADS),
                                                  in1=scores, op0=ALU.is_le, op1=ALU.mult))
                    step(dve.tensor_scalar(scores, scores, -1.0, -NEG_INF, ALU.add, ALU.mult))
                    for i in range(banks):
                        c, k = divmod(i, HEADS)
                        part = scores[:, c * 512:(c + 1) * 512]
                        dve.wait_ge(banks_ready[layer], t * banks + i + 1)
                        dve.tensor_scalar(chunk_b[:, :], ps_big[:, i % 2, :], head_bias[:, k:k + 1], None,
                                          ALU.add).then_inc(banks_used[layer], 1)
                        dve.wait_ge(banks_used[layer], t * banks + i + 3)
                        step(dve.scalar_tensor_tensor(out=chunk_a[:, 0:512], in0=chunk_b[:, :], scalar=SLOPE,
                                                      in1=chunk_b[:, :], op0=ALU.mult, op1=ALU.max))
                        step(dve.scalar_tensor_tensor(out=chunk_b[:, :], in0=adj_tile[:, c * 512:(c + 1) * 512],
                                                      scalar=float(k + 1), in1=chunk_a[:, 0:512],
                                                      op0=ALU.is_equal, op1=ALU.mult))
                        step(dve.tensor_tensor(part, part, chunk_b[:, :], ALU.add))
                if layer == 3:
                    dve.tensor_copy(queries[:, 0, :], hT_tile).then_inc(lhs_made[layer], 1)
                    dve.wait_ge(lhs_product[layer], t + 1)
                    dve.tensor_copy(f1_col[:, :], ps_t[:, 0:1]).then_inc(lhs_ready[layer], 1)
                    dve.wait_ge(lhs_ready[layer], t + 1)
                    dve.wait_ge(adj_in, 16 * (layer * T + t + 1))
                    step(dve.tensor_scalar(scores, adj_tile, 0.0, NEG_INF, ALU.is_le, ALU.mult))
                    for c in range(CH):
                        part = scores[:, c * 512:(c + 1) * 512]
                        dve.wait_ge(banks_ready[layer], t * banks + c + 1)
                        dve.tensor_scalar(chunk_b[:, :], ps_big[:, c % 2, :], f1_col[:, :], None,
                                          ALU.add).then_inc(banks_used[layer], 1)
                        dve.wait_ge(banks_used[layer], t * banks + c + 3)
                        step(dve.scalar_tensor_tensor(out=chunk_a[:, 0:512], in0=chunk_b[:, :], scalar=SLOPE,
                                                      in1=chunk_b[:, :], op0=ALU.mult, op1=ALU.max))
                        step(dve.scalar_tensor_tensor(out=chunk_b[:, :], in0=adj_tile[:, c * 512:(c + 1) * 512],
                                                      scalar=0.0, in1=chunk_a[:, 0:512], op0=ALU.is_gt, op1=ALU.mult))
                        step(dve.tensor_tensor(part, part, chunk_b[:, :], ALU.add))

            def dense():
                dve.wait_ge(x_again, 16)
                normalise(0)
                dve.sem_inc(quarters_used, 2)
                with step.loop(T, P * Q) as t:
                    dve.wait_ge(adj_in, 16 * (t + 1))
                    dve.tensor_scalar(mask_b, adj_tile, 0.0, None, ALU.not_equal).then_inc(mask_ready, 1)
                    dve.wait_ge(mask_ready, t + 1)
                    dve.sem_inc(adj_free, 1)
                    with step.loop(P, Q) as r:
                        for q in range(Q):
                            dve.wait_ge(quarters_ready, (t * P + r) * Q + q + 1)
                            dve.tensor_tensor(chunk_a[:, :],
                                              ps_big[:, 2 * (q % 2):2 * (q % 2) + 2, :].rearrange("p a b -> p (a b)"),
                                              hT[:, q * 1024:(q + 1) * 1024], ALU.mult).then_inc(quarters_used, 1)
                            dve.wait_ge(quarters_used, (t * P + r) * Q + q + 3)
                            step(dve.tensor_reduce(quarter_max[:, q:q + 1], chunk_a[:, :], AX.X, ALU.max))
                        dve.tensor_reduce(maxT[:, bass.ds(r, 1)], quarter_max[:, :], AX.X, ALU.max).then_inc(row_max_taken, 1)
                        dve.wait_ge(row_max_taken, t * P + r + 1)
                    dve.sem_inc(maxT_ready, 1)
                    dve.wait_ge(max_ready, t + 1)
                    dve.tensor_tensor(row_tile(xs, t), row_tile(xs, t), ps_t[:, 0:P], ALU.add).then_inc(x_updated, 1)
                    dve.wait_ge(x_updated, t + 1)

                STEPS = [0, 1 + 1, 3 + 3 * CH * HEADS + 1, 1 + 3 * CH + 1]
                FINISH = [0, 1, 0, 2]
                for layer in range(1, LAYERS):
                    normalise(layer)
                    dve.sem_inc(banks_used[layer], 2)
                    with step.loop(T, STEPS[layer] + FINISH[layer] + 1) as t:
                        dense_scores(layer, t)
                        step(dve.tensor_reduce(max_col[:, :], scores, AX.X, ALU.max))
                        dve.tensor_scalar(negmax[:, :], max_col[:, :], -1.0, None, ALU.mult).then_inc(rowmax_ready[layer], 1)
                        dve.sem_inc(adj_free, 1)
                        dve.wait_ge(probs_ready[layer], t + 1)
                        step(dve.reciprocal(rdenom[:, :], denom[:, :]))
                        dve.wait_ge(pv_done[layer], (t + 1) * CH)
                        dve.tensor_copy(u_tile[:, :], ps_acc[:, 0:D]).then_inc(u_copied[layer], 1)
                        dve.wait_ge(u_copied[layer], t + 1)
                        finish(layer, t, row_tile(xs, t))

            def sparse():
                all_slots = slots_of(T)
                for layer in range(LAYERS):
                    following = layer + 1
                    width = widths[layer]
                    if layer == 1:
                        dve.wait_ge(lhs_product[layer], 1)
                        dve.tensor_copy(queries[:, 0, :], ps_t[:, 0:P]).then_inc(lhs_ready[layer], 1)
                        dve.sem_inc(banks_used[layer], 2)
                        for c in range(CH):
                            dve.wait_ge(banks_ready[layer], c + 1)
                            dve.tensor_scalar(zero_scores[:, c * 512:(c + 1) * 512], ps_big[:, c % 2, :], -NEG_BIG, None,
                                              ALU.add).then_inc(banks_used[layer], 1)
                        dve.wait_ge(banks_used[layer], CH + 2)
                        dve.tensor_reduce(negmax[:, :], zero_scores, AX.X, ALU.max, negate=True)\
                            .then_inc(rowmax_ready[layer], 1)
                        dve.wait_ge(probs_ready[layer], 1)
                        step(dve.reciprocal(rdenom[:, :], denom[:, :]))
                        dve.wait_ge(pv_done[layer], CH)
                        dve.tensor_scalar(zero_row[:, :], ps_acc[:, 0:D], rdenom[:, :], None, ALU.mult)\
                            .then_inc(zero_ready, 1)
                        dve.wait_ge(zero_ready, 1)
                    if layer >= 2:
                        dve.wait_ge(rowT_ready[layer - 1], T)
                        step(dve.tensor_scalar(zero_row[:, :], ps_acc[:, 0:D], 1.0 / N, None, ALU.mult))

                    def gathered_rows(b, slots):
                        return gathered[b][:, 0:slots * width].rearrange("p (k w) -> p k w", w=width)

                    def score(t, b, slots, done):
                        g = gathered_rows(b, slots)
                        dve.wait_ge(gather_in[b], 16 * (done + layer * all_slots[b]))
                        if layer == 0:
                            dve.tensor_reduce(sum_s[:, b, :], g.rearrange("p k d -> p d k"), AX.X, ALU.max)\
                                .then_inc(gather_used, 1)
                            dve.wait_ge(gather_used, t + 1 + layer * T)
                            step(dve.tensor_tensor(row_tile(xs, t), row_tile(xs, t), sum_s[:, b, :], ALU.add), dve_passed)
                            return
                        sc, tmp = score_s[:, b, 0:slots], prob_s[:, b, 0:slots]
                        if layer < 3:
                            w = weighted[:, 0:slots * D].rearrange("p (k d) -> p k d", d=D)
                            step(dve.tensor_tensor(w, g, q_rows[:, bass.ds(t, 1), :].to_broadcast([P, slots, D]), ALU.mult))
                            step(dve.tensor_reduce(sc, w, AX.X, ALU.add))
                            if layer == 2:
                                step(dve.tensor_scalar(tmp, sc, head_bias[:, 0:1], None, ALU.add))
                        else:
                            step(dve.tensor_scalar(tmp, g[:, :, D], f1_rows[:, bass.ds(t, 1)], None, ALU.add))
                        if layer >= 2:
                            step(dve.scalar_tensor_tensor(out=sc, in0=tmp, scalar=SLOPE, in1=tmp, op0=ALU.mult, op1=ALU.max))
                        step(dve.tensor_tensor(sc, sc, row_tile(pad_bias, t)[:, 0:slots], ALU.add))
                        dve.tensor_reduce(negmax_s[:, b, :], sc, AX.X, ALU.max, negate=True).then_inc(sparse_scores[layer], 1)

                    def weigh(t, b, slots):
                        if layer == 0:
                            return
                        g = gathered_rows(b, slots)[:, :, 0:D]
                        w = weighted[:, 0:slots * D].rearrange("p (k d) -> p k d", d=D)
                        dve.wait_ge(sparse_probs[layer], t + 1)
                        step(dve.reciprocal(rdenom_s[:, b, :], denom_s[:, b, :]))
                        dve.tensor_tensor(w, g, prob_s[:, b, 0:slots].unsqueeze(2).to_broadcast([P, slots, D]), ALU.mult)\
                            .then_inc(gather_used, 1)
                        dve.wait_ge(gather_used, t + 1 + layer * T)
                        step(dve.tensor_reduce(sum_s[:, b, :], w.rearrange("p k d -> p d k"), AX.X, ALU.add))
                        step(dve.tensor_scalar(sum_s[:, b, :], sum_s[:, b, :], rdenom_s[:, b, :], None, ALU.mult))
                        dve.scalar_tensor_tensor(out=u_s[:, b, :], in0=zero_row[:, :], scalar=no_nbr[:, bass.ds(t, 1)],
                                                 in1=sum_s[:, b, :], op0=ALU.mult, op1=ALU.add).then_inc(u_ready[layer], 1)

                    def update(t, b, before_it):
                        x_tile = row_tile(xs, t)
                        delta = ps_delta[:, 0:D]
                        if layer == 1:
                            dve.wait_ge(delta_ready[layer], t + 1)
                            step(dve.tensor_tensor(sum_s[:, b, :], delta, b2_rows[:, :], ALU.add))
                            step(dve.scalar_tensor_tensor(out=x_tile, in0=sum_s[:, b, :], scalar=0.0, in1=x_tile,
                                                          op0=ALU.max, op1=ALU.add), dve_passed)
                        if layer == 2:
                            dve.wait_ge(u_ready[layer], t + 1)
                            step(dve.tensor_tensor(x_tile, x_tile, u_s[:, b, :], ALU.add), dve_passed)
                        if layer == 3:
                            dve.wait_ge(elu_exp[layer], t + 1)
                            step(dve.tensor_scalar(hid_s[:, b, :], hid_s[:, b, :], 1.0, -1.0, ALU.min, ALU.add))
                            step(dve.scalar_tensor_tensor(out=sum_s[:, b, :], in0=delta, scalar=0.0, in1=hid_s[:, b, :],
                                                          op0=ALU.max, op1=ALU.add))
                            if later(t):
                                dve.wait_ge(scattered[b], 16 * (before_it + layer * (T // 2)))
                            dve.tensor_copy(node_s[:, b, :], node_of(t))
                            dve.tensor_tensor(h_s[:, b, 0:D], x_tile, sum_s[:, b, :], ALU.add).then_inc(final_ready[layer], 1)
                            return
                        step(dve.bn_stats(bn_s[:, b, :], x_tile), dve_passed)
                        dve.bn_aggr(mv_s[:, b, :], bn_s[:, b, :]).then_inc(bn_ready[layer], 1)

                    def norm(t, b, before_it):
                        if following == LAYERS:
                            return
                        dve.wait_ge(row_std_ready[layer], t + 1)
                        step(dve.reciprocal(rstd_s[:, b, :], std_s[:, b, :]))
                        if later(t):
                            dve.wait_ge(scattered[b], 16 * (before_it + layer * (T // 2)))
                        dve.tensor_copy(node_s[:, b, :], node_of(t))
                        dve.scalar_tensor_tensor(out=shift_s[:, b, :], in0=mv_s[:, b, 0:1], scalar=-1.0,
                                                 in1=rstd_s[:, b, :], op0=ALU.mult, op1=ALU.mult)\
                            .then_inc(row_norm_ready[layer], 1)

                    def node_of(t):
                        return rows[:, bass.ds(t, 1), W_NODE:W_NODE + 1].rearrange("p o k -> p (o k)")

                    def prepare(t, b):
                        if following == 1:
                            dve.wait_ge(row_ready[layer], t + 1)
                            dve.tensor_copy(row_tile(hs, t), h_s[:, b, 0:D])
                            dve.wait_ge(rowT_copied[layer], t + 1)
                            dve.tensor_copy(hT[:, bass.ds(t * P, P)], ps_hT[:, 0:P]).then_inc(row_used[layer], 1)
                        if following == 2:
                            dve.wait_ge(row_ready[layer], t + 1)
                            dve.tensor_tensor(row_tile(q_rows, t), h_s[:, b, 0:D], w0_rows[:, :], ALU.mult)\
                                .then_inc(row_used[layer], 1)

                    def body(t, b, half, slots, done):
                        first = isinstance(t, int) and t == 0
                        score(t, b, slots, done)
                        before_it = half if b == 0 else half
                        if b == 0:
                            before_it = half - 1
                        if not first:
                            update(t - 1, 1 - b, before_it)
                        weigh(t, b, slots)
                        if not first:
                            norm(t - 1, 1 - b, before_it)
                            prepare(t - 1, 1 - b)

                    per_pair = [6, 20, 22, 16][layer]
                    over_tiles(body, lambda count, first: step.loop(count, per_pair, first), T)
                    update(T - 1, 1, T // 2 - 1)
                    norm(T - 1, 1, T // 2 - 1)
                    prepare(T - 1, 1)

            row_stats()
            layer_stats(0)
            find_neighbours()
            sort_rows()
            dve.wait_ge(flag_ready, 1)
            chained = step.n
            bad = dve.value_load(bad_flag[0:1, 0:1])
            with dve.If(bad > 0):
                dense()
            step.n = chained
            with dve.Else():
                sparse()


_INS = ['x', 'adj', 'L1_gnn_Wq', 'L1_gnn_Wk', 'L1_gnn_Wv', 'L1_gnn_W1', 'L1_gnn_b1', 'L1_gnn_W2', 'L1_gnn_b2',
        'L2_gnn_W', 'L2_gnn_b', 'L3_gnn_W', 'L3_gnn_a']
_OUTS = [((4096, 128), 'float32')]


def kernel(**inputs):
    import numpy as _np
    import concourse.bacc as _bacc
    from concourse import mybir as _mybir
    from concourse.bass_utils import run_bass_kernel_spmd as _run

    nc = _bacc.Bacc("TRN2", target_bir_lowering=False, num_devices=1)
    arrays, args = {}, []
    for name in _INS:
        a = _np.ascontiguousarray(inputs[name])
        arrays[f"in_{name}_dram"] = a
        args.append(nc.dram_tensor(f"in_{name}_dram", a.shape, _mybir.dt.from_np(a.dtype), kind="ExternalInput").ap())
    for i, (shape, dtype) in enumerate(_OUTS):
        dt = _mybir.dt.from_np(_np.dtype(dtype))
        args.append(nc.dram_tensor(f"out_{i}_dram", shape, dt, kind="ExternalOutput").ap())
    build(nc, *args)
    r = _run(nc, [arrays], core_ids=[0])
    got = tuple(r.results[0][f"out_{i}_dram"] for i in range(len(_OUTS)))
    return got[0]
```

```python
from contextlib import ExitStack, contextmanager

import concourse.bass as bass
from concourse import mybir

F32 = mybir.dt.float32
BF16 = mybir.dt.bfloat16
I32 = mybir.dt.int32
U32 = mybir.dt.uint32
F16 = mybir.dt.float16
ALU = mybir.AluOpType
ACT = mybir.ActivationFunctionType
AX = mybir.AxisListType

P = 128
LN_EPS = 1e-5
NEG_BIG = 1.0e6
NEG_INF = -9.0e15
SLOPE = 0.2
HEADS = 4
LAYERS = 4
SLOTS = 24
GROUP = 512
TOP = 8
PAD_BIAS = -1.0e30
RUNS = [(0, 23), (1, 15), (2, 13), (4, 12), (6, 11), (8, 10), (10, 9), (16, 8), (20, 7), (24, 6), (28, 5), (30, 4)]
EARLY = 10
LONGER = next(first for first, slots in RUNS if slots <= EARLY)
W_NODE = SLOTS
W_X = 32


def wait_alone(eng, sem, value, passed):
    eng.wait_ge(sem, value)
    eng.sem_inc(passed, 1)


class Chain:

    def __init__(self, eng, sem):
        self.eng, self.sem, self.n, self.steps = eng, sem, 0, 0

    def __call__(self, ins, passed=None):
        ins.then_inc(self.sem, 1)
        self.n = self.n + 1
        self.steps += 1
        if passed is None:
            self.eng.wait_ge(self.sem, self.n)
        else:
            wait_alone(self.eng, self.sem, self.n, passed)

    def mark(self, ins):
        ins.then_inc(self.sem, 1)
        self.n = self.n + 1
        self.steps += 1
        return self.n

    @contextmanager
    def loop(self, count, steps, first=0):
        start, seen = self.n, self.steps
        with self.eng.Fori(first, first + count) as i:
            self.n = start + (i - first) * steps
            yield i
        self.n = start + count * steps
        assert self.steps - seen == steps, (self.steps - seen, steps)
        self.steps = seen + count * steps


def later(t):
    return not (isinstance(t, int) and t < 2)


def slots_in_layer(slots, layer):
    return max(slots - EARLY, 0) if layer == 0 else slots


def over_tiles(body, loop, tiles, layer):
    total = slots_before(layer, tiles)
    ends = [first for first, _ in RUNS[1:]] + [tiles]
    for (first, all_slots), end in zip(RUNS, ends):
        slots = slots_in_layer(all_slots, layer)
        if not slots:
            continue
        if end - first <= 2:
            for t in range(first, end):
                total[t % 2] += slots
                body(t, t % 2, t // 2, slots, total[t % 2])
            continue
        with loop((end - first) // 2, first // 2, slots) as half:
            for b in range(2):
                done = (half - (first // 2 - 1)) * slots + total[b]
                body(2 * half + b, b, half, slots, done)
        for b in range(2):
            total[b] += (end - first) // 2 * slots


def slots_before(layer, tiles):
    total = [0, 0]
    ends = [first for first, _ in RUNS[1:]] + [tiles]
    for earlier in range(layer):
        for (first, slots), end in zip(RUNS, ends):
            for t in range(first, end):
                total[t % 2] += slots_in_layer(slots, earlier)
    return total


def tiles_before(layer, tiles):
    return LONGER + (layer - 1) * tiles if layer else 0


def build(nc, x, adj, Wq, Wk, Wv, W1, b1, W2, b2, W2h, b2h, W3, a3, out):
    N, D = x.shape
    T = N // P
    CH = N // 512
    Q = N // 1024
    x_rows = x.rearrange("(t p) d -> p t d", p=P)
    out_rows = out.rearrange("(t p) d -> p t d", p=P)

    with ExitStack() as ctx:
        def sb(name, shape, dt=F32):
            return ctx.enter_context(nc.sbuf_tensor(name, shape, dt))

        def pb(name, shape):
            return ctx.enter_context(nc.psum_tensor(name, shape, F32))

        def sem(name):
            return ctx.enter_context(nc.semaphore(name))

        wq, wk, wv, w1, w2, w3 = (sb(n, [P, D]) for n in ("wq", "wk", "wv", "w1", "w2", "w3"))
        wT = sb("wT", [P, 4, D])
        a_cols = sb("a_cols", [P, 2])
        b1_col = sb("b1_col", [P, 1])
        b2_rows = sb("b2_rows", [P, D])
        head_cols = sb("head_cols", [P, HEADS])
        head_bias = sb("head_bias", [P, HEADS])
        w_qk = sb("w_qk", [P, D])
        w_v1 = sb("w_v1", [P, D])
        w_a = sb("w_a", [P, 2])
        w_a2 = sb("w_a2", [P, P])
        ones = sb("ones", [P, P])
        ident = sb("ident", [P, P])
        ident_b = sb("ident_b", [P, P], BF16)

        rows = sb("rows", [P, T, W_X + 2 * D], U32)
        xs = rows[:, :, W_X:W_X + D].bitcast(F32)
        early_max = rows[:, :, W_X + D:].bitcast(F32)
        hs_rows = sb("hs_rows", [P, T, D + 1])
        hs = hs_rows[:, :, 0:D]
        hT = sb("hT", [P, N])
        stats = sb("stats", [P, T, 6])
        mean, gap, var = sb("mean", [P, T]), sb("gap", [P, T]), sb("var", [P, T])
        std, rstd, shift = sb("std", [P, T]), sb("rstd", [P, T]), sb("shift", [P, T])
        h_tile = sb("h_tile", [P, D])
        u_tile = sb("u_tile", [P, D])
        uT_tile = sb("uT_tile", [P, P])
        hid_tile = sb("hid_tile", [P, P])
        sum_tile = sb("sum_tile", [P, D])
        max_col = sb("max_col", [P, 1])
        negmax = sb("negmax", [P, 1])
        denom = sb("denom", [P, 1])
        rdenom = sb("rdenom", [P, 1])

        adj_bufs = sb("adj_bufs", [P, 3, N], I32)
        work = sb("work", [P, 3, N])

        adj_tile = adj_bufs[:, 0, :]
        scores = work[:, 0, :]
        probs = work[:, 1, :]
        mask_b = work[:, 2, 0:N // 2].bitcast(BF16)
        chunk_a = sb("chunk_a", [P, 1024])
        chunk_b = sb("chunk_b", [P, 512])
        pT = sb("pT", [P, 2, 512])
        queries = sb("queries", [P, HEADS, P])

        key = work[:, 0, 0:N // 2].bitcast(F16)
        halves = [work[:, i, N // 2:].bitcast(F16) for i in (0, 2)]
        early_rows = work[:, 1, 0:2 * EARLY * D].rearrange("p (b k d) -> p b k d", b=2, d=D)
        xs_early = work[:, 1, :].rearrange("p (t d) -> p t d", d=D)
        early_slots = sb("early_slots", [P, 2, SLOTS], U32)
        G8 = N // GROUP * TOP
        iota_g = work[:, 2, 0:N // 2].bitcast(F16)
        group_first = sb("group_first", [P, G8])
        offset = sb("offset", [P, G8])
        cand = sb("cand", [P, 2, 2, G8])
        top24 = sb("top24", [P, 2, SLOTS])
        pad_bias = sb("pad_bias", [P, T, SLOTS])
        group_full = sb("group_full", [P, T])
        square_sums = sb("square_sums", [P, T])
        weight_squares = sb("weight_squares", [P, 8])
        totals = sb("totals", [P, 8])
        minus_half = sb("minus_half", [P, 1])
        bad_cols = sb("bad_cols", [P, 8 + len(RUNS)])
        bad_col = sb("bad_col", [P, 1])
        bad_flag = sb("bad_flag", [P, 1], I32)
        small = sb("small", [P, 4])

        C = SLOTS + 1
        CT = C * T
        degree = sb("degree", [P, T])
        class_iota = hT[:, N // 4:N // 4 + CT]
        onehot = work[:, 0, CT:2 * CT]
        run_sum = [work[:, 0, 2 * CT:3 * CT], work[:, 0, 3 * CT:4 * CT]]
        class_total = work[:, 0, 4 * CT:5 * CT]
        filled = work[:, 2, 0:T * SLOTS]
        onehot_b = sb("onehot_b", [P, CT], BF16)
        before_b = sb("before_b", [P, P], BF16)
        ones_b = sb("ones_b", [P, P], BF16)
        place = sb("place", [P, T])
        place_u = sb("place_u", [P, T], U32)

        W3R = D + 1
        gathered = [work[:, 0, :], work[:, 1, :]]
        weighted = work[:, 2, :]
        q_rows = adj_bufs[:, 2, :].bitcast(F32).rearrange("p (t d) -> p t d", d=D)
        zero_scores = adj_bufs[:, 0, :].bitcast(F32)
        zero_probs = adj_bufs[:, 1, :].bitcast(F32)
        no_nbr = sb("no_nbr", [P, T])
        f1_rows = sb("f1_rows", [P, T])
        zero_row = sb("zero_row", [P, D])
        w0_rows = sb("w0_rows", [P, D])
        table_pad = sb("table_pad", [1, W3R])
        eps_col = sb("eps_col", [P, 1])
        unused = sb("unused", [P, 1])
        slots_s = sb("slots_s", [P, 2, SLOTS], U32)
        node_s = sb("node_s", [P, 2, 1], U32)
        score_s = sb("score_s", [P, 2, SLOTS])
        prob_s = sb("prob_s", [P, 2, SLOTS])
        negmax_s = sb("negmax_s", [P, 2, 1])
        denom_s = sb("denom_s", [P, 2, 1])
        rdenom_s = sb("rdenom_s", [P, 2, 1])
        u_s = sb("u_s", [P, 2, D])
        uT_s = sb("uT_s", [P, 2, P])
        hid_s = sb("hid_s", [P, 2, P])
        sum_s = sb("sum_s", [P, 2, D])
        sum_d = sb("sum_d", [P, D])
        bn_s = sb("bn_s", [P, 2, 6])
        mv_s = sb("mv_s", [P, 2, 2])
        std_s = sb("std_s", [P, 2, 1])
        rstd_s = sb("rstd_s", [P, 2, 1])
        shift_s = sb("shift_s", [P, 2, 1])
        h_s = sb("h_s", [P, 2, W3R])
        hT_s = sb("hT_s", [P, 2, P])
        widths = [D, W3R, D, W3R]
        place_no = sb("place_no", [P, T])
        tables = [nc.dram_tensor(f"table{layer}", (N + 1, widths[layer]), F32).ap() for layer in range(LAYERS)]
        sorted_rows = nc.dram_tensor("sorted_rows", (N, W_X + 2 * D), U32).ap()
        f1_col = sb("f1_col", [P, 1])
        quarter_max = sb("quarter_max", [P, Q])
        maxT = sb("maxT", [P, P])

        ps_big = pb("ps_big", [P, 4, 512])
        ps_t = pb("ps_t", [P, 512])
        ps_acc = pb("ps_acc", [P, 512])
        ps_e = pb("ps_e", [P, 512])
        ps_f = pb("ps_f", [P, 512])
        square_out = hT[:, N // 2:].bitcast(BF16)
        ps_uT, ps_hid, ps_delta, ps_hT = (ps_big[:, i, :] for i in range(4))

        x_in = sem("x_in")
        weights_in = sem("weights_in")
        ident_zeroed = sem("ident_zeroed")
        ident_ready = sem("ident_ready")
        wT_ready = sem("wT_ready")
        wT_copied = sem("wT_copied")
        products_ready = sem("products_ready")
        products_copied = sem("products_copied")
        dve_step = sem("dve_step")
        out_done = sem("out_done")

        def sems(name, *layers):
            return {layer: sem(f"{name}{layer}") for layer in layers or range(LAYERS)}

        norm_ready = sems("norm_ready")
        h_ready = sems("h_ready")
        var_ready = sems("var_ready")
        std_ready = sems("std_ready")
        hT_ready = sems("hT_ready")
        h_stored = sems("h_stored")
        adj_in = sem("adj_in")
        adj_free = sem("adj_free")
        u_ready = sems("u_ready", 1, 2, 3)
        uT_ready = sems("uT_ready", 1, 3)
        uT_copied = sems("uT_copied", 1, 3)
        hid_ready = sems("hid_ready", 1)
        hid_copied = sems("hid_copied", 1)
        delta_ready = sems("delta_ready", 1, 3)
        elu_in = sems("elu_in", 3)
        elu_exp = sems("elu_exp", 3)
        x_updated = sem("x_updated")
        mask_ready = sem("mask_ready")
        quarters_ready = sem("quarters_ready")
        quarters_used = sem("quarters_used")
        maxT_ready = sem("maxT_ready")
        max_ready = sem("max_ready")
        row_max_taken = sem("row_max_taken")
        u_copied = sems("u_copied", 1, 2, 3)
        lhs_made = sems("lhs_made", 3)
        lhs_product = sems("lhs_product", 1, 3)
        lhs_ready = sems("lhs_ready", 1, 2, 3)
        banks_ready = sems("banks_ready", 1, 2, 3)
        banks_used = sems("banks_used", 1, 2, 3)
        rowmax_ready = sems("rowmax_ready", 1, 2, 3)
        probs_ready = sems("probs_ready", 1, 2, 3)
        pT_ready = sems("pT_ready", 1, 2, 3)
        pT_copied = sems("pT_copied", 1, 2, 3)
        pv_done = sems("pv_done", 1, 2, 3)

        consts_ready = sem("consts_ready")
        pads_in = sem("pads_in")
        scan_in = [sem("scan_in_even"), sem("scan_in_odd")]
        keys_made = sem("keys_made")
        halves_ready = sem("halves_ready")
        squares_done = sem("squares_done")
        weights_squared = sem("weights_squared")
        onehot_ready = sem("onehot_ready")
        prefix_ready = sem("prefix_ready")
        places_ready = sem("places_ready")
        rows_scattered = sem("rows_scattered")
        rows_sorted = sem("rows_sorted")
        bad_ready = sem("bad_ready")
        bad_summed = sem("bad_summed")
        flag_ready = sem("flag_ready")
        tables_in = sem("tables_in")
        finished_ready = sem("finished_ready")
        slots_in = [sem(f"slots_in{b}") for b in range(2)]
        gather_in = [sem(f"gather_in{b}") for b in range(2)]
        gather_used = sem("gather_used")
        bn_ready = sems("bn_ready", 0, 1, 2)
        row_std_ready = sems("row_std_ready", 0, 1, 2)
        row_norm_ready = sems("row_norm_ready", 0, 1, 2)
        row_ready = sems("row_ready", 0, 1, 2)
        scattered = [sem(f"scattered{b}") for b in range(2)]
        written = [sem(f"written{b}") for b in range(2)]
        rowT_ready = sems("rowT_ready", 0, 1, 2)
        rowT_copied = sems("rowT_copied", 0, 2)
        row_q_ready = sems("row_q_ready", 0, 2)
        row_used = sems("row_used", 0, 1)
        sparse_scores = sems("sparse_scores", 1, 2, 3)
        sparse_probs = sems("sparse_probs", 1, 2, 3)
        zero_ready = sem("zero_ready")
        q_copied = sems("q_copied", 0, 2)
        x_again = sem("x_again")
        table0_ready = sem("table0_ready")
        pad_row_ready = sem("pad_row_ready")
        node_zeroed = sem("node_zeroed")
        node_ready = sem("node_ready")
        iota_ready = sem("iota_ready")
        classes_ready = sem("classes_ready")
        dve_passed = sem("dve_passed")
        pool_passed = sem("pool_passed")
        early_found = sem("early_found")
        early_in = [sem(f"early_in{b}") for b in range(2)]
        early_used = sem("early_used")
        final_ready = sems("final_ready", 3)

        block = ctx.enter_context(nc.Block())
        WEIGHTS = 16 * 13
        heads = [0, 1, HEADS, 1]

        @block.sync
        def _(sp):
            sp.dma_start(xs, x_rows).then_inc(x_in, 16)
            for dst, src in ((wq, Wq), (wk, Wk), (wv, Wv), (w1, W1), (w2, W2), (w3, W3)):
                sp.dma_start(dst[:, :], src).then_inc(weights_in, 16)
            for c in range(2):
                sp.dma_start(a_cols[:, c:c + 1], a3[c * D:(c + 1) * D, :]).then_inc(weights_in, 16)
            sp.dma_start(b1_col[:, :], b1.rearrange("(p o) -> p o", o=1)).then_inc(weights_in, 16)
            sp.dma_start(b2_rows[:, :], b2.partition_broadcast(P)).then_inc(weights_in, 16)
            sp.dma_start(head_cols[:, :], W2h.rearrange("k d -> d k"), allow_slow_non_contiguous=True).then_inc(weights_in, 16)
            sp.dma_start(head_bias[:, :], b2h.partition_broadcast(P)).then_inc(weights_in, 16)
            sp.dma_start(w0_rows[:, :], W2h[0, :].partition_broadcast(P)).then_inc(weights_in, 16)
            for b in range(2):
                sp.dma_start(adj_bufs[:, b, :], adj[b * P:(b + 1) * P, :]).then_inc(scan_in[b], 16)
            sp.wait_ge(pad_row_ready, 1)
            for layer in range(LAYERS):
                sp.dma_start(tables[layer][0:1, :], table_pad[:, 0:widths[layer]]).then_inc(pads_in, 16)
            table0 = tables[0][1:N + 1, :].rearrange("(t p) d -> p t d", p=P)
            for first in range(0, T, T // 4):
                end = first + T // 4
                sp.wait_ge(table0_ready, end)
                sp.dma_start(table0[:, first:end, :], hs[:, first:end, :]).then_inc(tables_in, 16)
            with sp.Fori(1, T // 2) as half:
                for b in range(2):
                    sp.wait_ge(halves_ready, 2 * half + b - 1)
                    sp.wait_ge(squares_done, 2 * half + b - 1)
                    sp.dma_start(adj_bufs[:, b, :], adj[bass.ds((2 * half + b) * P, P), :]).then_inc(scan_in[b], 16)
            sp.wait_ge(finished_ready, T)
            sp.dma_start(tables[1][1:N + 1, :].rearrange("(t p) d -> p t d", p=P), hs_rows[:, :, :]).then_inc(tables_in, 16)
            sp.wait_ge(rows_scattered, 16 * T)
            for b in range(2):
                sp.dma_start(slots_s[:, b, :], sorted_rows[b * P:(b + 1) * P, 0:SLOTS]).then_inc(slots_in[b], 16)
            by_place = sorted_rows.rearrange("(t p) w -> p t w", p=P)
            sp.dma_start(rows[:, :, :], by_place).then_inc(rows_sorted, 16)

            sp.wait_ge(tables_in, 16 * 5)
            sp.wait_ge(pads_in, 16 * LAYERS)

            def sparse():
                sp.wait_ge(rows_sorted, 16)
                for layer in range(LAYERS):
                    ready = {1: row_ready, 2: q_copied}.get(layer)

                    def write(t, b):
                        sp.wait_ge(ready[layer], t + 1)
                        sp.dma_start(tables[layer + 1][bass.ds(t * P + 1, P), :], h_s[:, b, 0:widths[layer + 1]])\
                            .then_inc(written[b], 16)

                    def body(t, b, half, slots, done):
                        if layer == 0 and not later(t):
                            return
                        if not later(t):
                            if layer == 2:
                                sp.wait_ge(gather_used, tiles_before(2, T))
                            if layer:
                                sp.wait_ge(gather_in[b], 16 * slots_before(layer, T)[b])
                        else:
                            sp.wait_ge(gather_in[b], 16 * (done - slots))
                        sp.dma_start(slots_s[:, b, :], rows[:, bass.ds(t, 1), 0:SLOTS].rearrange("p o k -> p (o k)"))\
                            .then_inc(slots_in[b], 16)
                        if ready and not (isinstance(t, int) and t < 3):
                            write(t - 3, 1 - b)

                    over_tiles(body, lambda count, first, slots: sp.Fori(first, first + count), T, layer)
                    if ready:
                        write(T - 3, 1)
                        write(T - 2, 0)
                        write(T - 1, 1)
                for b in range(2):
                    sp.wait_ge(scattered[b], 16 * (LONGER // 2 + T // 2))

            def dense():
                sp.wait_ge(rows_sorted, 16)
                for b in range(2):
                    sp.wait_ge(slots_in[b], 16)
                sp.dma_start(xs, x_rows).then_inc(x_again, 16)
                for layer in range(LAYERS):
                    if layer:
                        sp.wait_ge(adj_free, layer * T)
                    sp.dma_start(adj_tile, adj[0:P, :]).then_inc(adj_in, 16)
                    with sp.Fori(1, T) as t:
                        sp.wait_ge(adj_free, layer * T + t)
                        sp.dma_start(adj_tile, adj[bass.ds(t * P, P), :]).then_inc(adj_in, 16)
                sp.wait_ge(x_updated, LAYERS * T)
                sp.dma_start(out_rows, xs).then_inc(out_done, 16)
                sp.wait_ge(out_done, 16)

            sp.wait_ge(flag_ready, 1)
            bad = sp.value_load(bad_flag[0:1, 0:1])
            with sp.If(bad > 0):
                dense()
            with sp.Else():
                sparse()

        @block.gpsimd
        def _(pool):
            pool.memset(ident[:, :], 0.0).then_inc(ident_zeroed, 1)
            pool.memset(ident_b[:, :], 0.0).then_inc(ident_zeroed, 1)
            pool.memset(ones_b[:, :], 1.0).then_inc(ident_zeroed, 1)
            pool.memset(ones[:, :], 1.0).then_inc(ident_ready, 1)
            pool.wait_ge(ident_zeroed, 3)
            for m in (ident, ident_b):
                pool.affine_select(out=m[:, :], in_=m[:, :], compare_op=ALU.not_equal, fill=1.0, base=0,
                                   pattern=[[-1, P]], channel_multiplier=1).then_inc(ident_ready, 1)
            pool.memset(weight_squares[:, :], 0.0).then_inc(consts_ready, 1)
            pool.memset(minus_half[:, :], -0.5).then_inc(consts_ready, 1)
            pool.memset(eps_col[:, :], LN_EPS).then_inc(consts_ready, 1)
            pool.memset(bad_cols[:, :], 0.0).then_inc(consts_ready, 1)
            pool.affine_select(out=before_b[:, :], in_=ones_b[:, :], compare_op=ALU.is_gt, fill=0.0, base=0,
                               pattern=[[1, P]], channel_multiplier=-1).then_inc(consts_ready, 1)
            pool.iota(iota_g, [[0, N // GROUP], [1, GROUP]], base=1, channel_multiplier=0,
                      allow_small_or_imprecise_dtypes=True).then_inc(iota_ready, 1)
            pool.iota(group_first[:, :], [[GROUP, N // GROUP], [0, TOP]], base=0, channel_multiplier=0,
                      allow_small_or_imprecise_dtypes=True).then_inc(iota_ready, 1)
            pool.iota(place_no[:, :], [[P, T]], base=1, channel_multiplier=1,
                      allow_small_or_imprecise_dtypes=True).then_inc(iota_ready, 1)
            pool.memset(table_pad[:, :], 0.0).then_inc(pad_row_ready, 1)
            pool.memset(rows[:, :, SLOTS:W_X], 0).then_inc(node_zeroed, 1)
            pool.wait_ge(node_zeroed, 1)
            pool.iota(rows[:, :, W_NODE:W_NODE + 1], [[P, T], [0, 1]], base=1, channel_multiplier=1).then_inc(node_ready, 1)

            pool.iota(class_iota.rearrange("p (c t) -> p c t", t=T), [[-1, C], [0, T]], base=SLOTS,
                      channel_multiplier=0, allow_small_or_imprecise_dtypes=True).then_inc(classes_ready, 1)

            pool.wait_ge(tables_in, 16 * 4)
            pool.wait_ge(pads_in, 16 * LAYERS)
            with pool.Fori(0, T // 2) as half:
                for b in range(2):
                    pool.wait_ge(early_used, 2 * half + b + 1)
                    wait_alone(pool, early_found, 2 * half + b + 1, pool_passed)
                    for k in range(EARLY):
                        pool.indirect_dma_start(early_rows[:, b, k, :], None, tables[0],
                                                bass.IndirectOffsetOnAxis(ap=early_slots[:, b, k:k + 1], axis=0))\
                            .then_inc(early_in[b], 16)

            pool.wait_ge(node_ready, 1)
            pool.wait_ge(places_ready, 1)
            pool.wait_ge(early_used, T + 2)
            for t in range(T):
                pool.indirect_dma_start(sorted_rows, bass.IndirectOffsetOnAxis(ap=place_u[:, t:t + 1], axis=0),
                                        rows[:, t, :], None).then_inc(rows_scattered, 16)

            def sparse():
                for layer in range(LAYERS):
                    width = widths[layer]
                    if layer:
                        for b in range(2):
                            if layer == 1:
                                pool.wait_ge(scattered[b], 16 * (LONGER // 2))
                            else:
                                pool.wait_ge(written[b], 16 * (layer - 1) * (T // 2))
                    ready = final_ready[3] if layer == 3 else row_ready[0]

                    def scatter(t, b):
                        wait_alone(pool, ready, t + 1, pool_passed)
                        last = layer == LAYERS - 1
                        dst, columns = (out, D) if last else (tables[layer + 1], widths[layer + 1])
                        pool.indirect_dma_start(dst, bass.IndirectOffsetOnAxis(ap=node_s[:, b, :], axis=0),
                                                h_s[:, b, 0:columns], None).then_inc(scattered[b], 16)

                    first_slot = EARLY if layer == 0 else 0

                    def body(t, b, half, slots, done):
                        if later(t):
                            pool.wait_ge(gather_used, t - 1 + tiles_before(layer, T))
                        wait_alone(pool, slots_in[b], 16 * (half + 1 + tiles_before(layer, T) // 2), pool_passed)
                        for k in range(first_slot, first_slot + slots):
                            pool.indirect_dma_start(gathered[b][:, (k - first_slot) * width:(k - first_slot + 1) * width], None, tables[layer],
                                                    bass.IndirectOffsetOnAxis(ap=slots_s[:, b, k:k + 1], axis=0))\
                                .then_inc(gather_in[b], 16)
                        if layer in (0, 3) and not (isinstance(t, int) and t < 3):
                            scatter(t - 3, 1 - b)

                    over_tiles(body, lambda count, first, slots: pool.Fori(first, first + count), T, layer)
                    if layer in (1, 2):
                        continue
                    tiles = LONGER if layer == 0 else T
                    scatter(tiles - 3, 1)
                    scatter(tiles - 2, 0)
                    scatter(tiles - 1, 1)

            pool.wait_ge(tables_in, 16 * 5)
            pool.wait_ge(flag_ready, 1)
            bad = pool.value_load(bad_flag[0:1, 0:1])
            with pool.If(bad > 0):
                pool.wait_ge(x_again, 16)
            with pool.Else():
                sparse()

        @block.tensor
        def _(pe):
            pe.wait_ge(ident_ready, 3)
            pe.wait_ge(weights_in, WEIGHTS)
            for i, w in enumerate((wq, wk, wv, w3)):
                mm = pe.transpose(ps_t[:, i * P:(i + 1) * P], w[:, :], ident[:, :])
            mm.then_inc(wT_ready, 1)
            pe.wait_ge(wT_copied, 1)
            pe.matmul(ps_e[:, 0:D], wT[:, 0, :], wT[:, 1, :], start=True, stop=True)
            pe.matmul(ps_acc[:, 0:D], wT[:, 2, :], w1[:, :], start=True, stop=True)
            pe.matmul(ps_f[:, 0:2], wT[:, 3, :], a_cols[:, :], start=True, stop=True)
            pe.wait_ge(weights_squared, 6)
            pe.matmul(ps_f[:, 64:72], ones[:, :], weight_squares[:, :], start=True, stop=True).then_inc(products_ready, 1)
            pe.wait_ge(products_copied, 1)

            pe.wait_ge(consts_ready, 5)
            pe.wait_ge(onehot_ready, 1)
            h2 = CT // 2
            for i in range(2):
                pe.matmul(ps_big[:, i, 0:h2], before_b[:, :], onehot_b[:, i * h2:(i + 1) * h2], start=True, stop=True)
            for i in range(2):
                mm = pe.matmul(ps_big[:, 2 + i, 0:h2], ones_b[:, :], onehot_b[:, i * h2:(i + 1) * h2],
                               start=True, stop=True)
            mm.then_inc(prefix_ready, 1)
            pe.wait_ge(bad_ready, 1)
            pe.matmul(ps_f[:, 0:1], ones[:, :], bad_col[:, :], start=True, stop=True).then_inc(bad_summed, 1)

            def transpose_rows(layer):
                with pe.Fori(0, T) as t:
                    pe.wait_ge(h_ready[layer], t + 1)
                    pe.transpose(ps_t[:, 0:P], h_tile[:, :], ident[:, :]).then_inc(hT_ready[layer], 1)
                pe.wait_ge(h_stored[layer], T + 1)

            def finish(layer, n):
                if layer == 2:
                    return
                pe.wait_ge(u_ready[layer], n + 1)
                pe.transpose(ps_e[:, 0:P], u_tile[:, :], ident[:, :]).then_inc(uT_ready[layer], 1)
                pe.wait_ge(uT_copied[layer], n + 1)
                if layer == 1:
                    pe.matmul(ps_f[:, 0:P], w_v1[:, :], uT_tile[:, :], start=True, stop=True).then_inc(hid_ready[layer], 1)
                    pe.wait_ge(hid_copied[layer], n + 1)
                    pe.matmul(ps_e[:, 0:D], hid_tile[:, :], w2[:, :], start=True, stop=True).then_inc(delta_ready[layer], 1)
                else:
                    pe.matmul(ps_f[:, 0:D], uT_tile[:, :], w3[:, :], start=True, stop=True).then_inc(delta_ready[layer], 1)

            def attend(layer, t, lhs, probs):
                banks = CH * heads[layer]
                pe.wait_ge(lhs_ready[layer], t + 1)
                for i in range(banks):
                    c, k = divmod(i, heads[layer])
                    pe.wait_ge(banks_used[layer], t * banks + i + 1)
                    pe.matmul(ps_big[:, i % 2, :], lhs(k), hT[:, c * 512:(c + 1) * 512],
                              start=True, stop=True).then_inc(banks_ready[layer], 1)
                pe.wait_ge(probs_ready[layer], t + 1)
                for c in range(CH + 1):
                    if c < CH:
                        if c >= 2:
                            pe.wait_ge(pT_copied[layer], t * CH + c - 1)
                        for b in range(4):
                            j = c * 4 + b
                            mm = pe.transpose(ps_big[:, 2 + c % 2, b * P:(b + 1) * P],
                                              probs[:, j * P:(j + 1) * P], ident[:, :])
                        mm.then_inc(pT_ready[layer], 1)
                    if c:
                        pe.wait_ge(pT_copied[layer], t * CH + c)
                        for b in range(4):
                            j = (c - 1) * 4 + b
                            mm = pe.matmul(ps_acc[:, 0:D], pT[:, (c - 1) % 2, b * P:(b + 1) * P], hs[:, j, :],
                                           start=(j == 0), stop=(j == T - 1))
                        mm.then_inc(pv_done[layer], 1)

            def dense():
                transpose_rows(0)
                with pe.Fori(0, T) as t:
                    with pe.Fori(0, P) as r:
                        pe.wait_ge(mask_ready, t + 1)
                        for q in range(Q):
                            pe.wait_ge(quarters_used, (t * P + r) * Q + q + 1)
                            for half in range(2):
                                c = 2 * q + half
                                mm = pe.matmul(ps_big[:, 2 * (q % 2) + half, :],
                                               ident_b[:, bass.ds(r, 1)].to_broadcast([P, P]),
                                               mask_b[:, c * 512:(c + 1) * 512], start=True, stop=True)
                            mm.then_inc(quarters_ready, 1)
                    pe.wait_ge(maxT_ready, t + 1)
                    pe.transpose(ps_t[:, 0:P], maxT[:, :], ident[:, :]).then_inc(max_ready, 1)

                for layer in range(1, LAYERS):
                    transpose_rows(layer)
                    with pe.Fori(0, T) as t:
                        if layer == 1:
                            pe.matmul(ps_t[:, 0:P], w_qk[:, :], hT[:, bass.ds(t * P, P)], start=True,
                                      stop=True).then_inc(lhs_product[layer], 1)
                        if layer == 3:
                            pe.wait_ge(lhs_made[layer], t + 1)
                            pe.matmul(ps_t[:, 0:1], queries[:, 0, :], w_a[:, 0:1], start=True,
                                      stop=True).then_inc(lhs_product[layer], 1)
                        attend(layer, t, lambda k: w_a2[:, :] if layer == 3 else queries[:, k, :], probs)
                        finish(layer, t)

            def sparse():
                tiles, groups = LONGER, (T - LONGER) // 4
                for layer in range(LAYERS):
                    following = layer + 1
                    if layer == 1:
                        pe.wait_ge(row_used[0], tiles + groups)
                        pe.wait_ge(q_copied[0], tiles + groups)
                        pe.matmul(ps_t[:, 0:P], w_qk[:, :], hT[:, N - P:N], start=True, stop=True)\
                            .then_inc(lhs_product[layer], 1)
                        attend(layer, 0, lambda k: queries[:, 0, :], zero_probs)
                        pe.wait_ge(zero_ready, 1)

                    def finish_first(t, b):
                        if layer in (1, 3):
                            pe.wait_ge(u_ready[layer], t + 1)
                            pe.transpose(ps_uT[:, 0:P], u_s[:, b, :], ident[:, :]).then_inc(uT_ready[layer], 1)
                            pe.wait_ge(uT_copied[layer], t + 1)
                            if layer == 1:
                                pe.matmul(ps_hid[:, 0:P], w_v1[:, :], uT_s[:, b, :], start=True,
                                          stop=True).then_inc(hid_ready[layer], 1)
                            else:
                                pe.matmul(ps_delta[:, 0:P], uT_s[:, b, :], w3[:, :], start=True,
                                          stop=True).then_inc(delta_ready[layer], 1)

                    def finish_last(t, b):
                        if layer == 1:
                            pe.wait_ge(hid_copied[layer], t + 1)
                            pe.matmul(ps_delta[:, 0:D], hid_s[:, b, :], w2[:, :], start=True,
                                      stop=True).then_inc(delta_ready[layer], 1)

                    def prepare(t, b):
                        if following == LAYERS:
                            return
                        pe.wait_ge(row_ready[layer], t + 1)
                        if following >= 2:
                            mm = pe.matmul(ps_acc[:, 0:D], ones[:, :], h_s[:, b, 0:D],
                                           start=isinstance(t, int) and t == 0, stop=isinstance(t, int) and t == T - 1)
                        if following != 2:
                            if following == 1 and not (isinstance(t, int) and t == 0):
                                pe.wait_ge(row_used[layer], t)
                            mm = pe.transpose(ps_hT[:, 0:P], h_s[:, b, 0:D], ident[:, :])
                        mm.then_inc(rowT_ready[layer], 1)
                        if following != 2:
                            pe.wait_ge(rowT_copied[layer], t + 1)
                            if not (isinstance(t, int) and t == 0):
                                pe.wait_ge(q_copied[layer], t)
                            columns, w = (D, w_qk) if following == 1 else (2, w_a)
                            pe.matmul(ps_t[:, 0:columns], hT_s[:, b, :], w[:, 0:columns], start=True,
                                      stop=True).then_inc(row_q_ready[layer], 1)

                    def body(t, b, half, slots, done):
                        if layer == 1:
                            finish_first(t, b)
                        if not (isinstance(t, int) and t == 0):
                            prepare(t - 1, 1 - b)
                        if layer != 1:
                            finish_first(t, b)
                        finish_last(t, b)

                    over_tiles(body, lambda count, first, slots: pe.Fori(first, first + count), T, layer)
                    prepare((LONGER if layer == 0 else T) - 1, 1)
                    if layer == 0:
                        pe.wait_ge(row_used[0], LONGER)
                        for n in range(groups + 1):
                            if n < groups:
                                if n >= 2:
                                    pe.wait_ge(row_used[0], tiles + n - 1)
                                pe.wait_ge(finished_ready, T + 4 * (n + 1))
                                for i in range(4):
                                    mm = pe.transpose(ps_big[:, n % 2, i * P:(i + 1) * P], hs[:, tiles + 4 * n + i, :], ident[:, :])
                                mm.then_inc(rowT_ready[0], 1)
                            if n:
                                pe.wait_ge(row_used[0], tiles + n)
                                if n >= 3:
                                    pe.wait_ge(q_copied[0], tiles + n - 2)
                                for i in range(4):
                                    at = (tiles + 4 * (n - 1) + i) * P
                                    mm = pe.matmul(ps_big[:, 2 + n % 2, i * P:(i + 1) * P], hT[:, at:at + P], w_qk[:, :],
                                                   start=True, stop=True)
                                mm.then_inc(row_q_ready[0], 1)

            pe.wait_ge(flag_ready, 1)
            bad = pe.value_load(bad_flag[0:1, 0:1])
            with pe.If(bad > 0):
                dense()
            with pe.Else():
                sparse()

        @block.scalar
        def _(act):
            def row_tile(a, t):
                return a[:, bass.ds(t, 1), :].rearrange("p o d -> p (o d)")

            def row_std(layer, passes=1):
                act.wait_ge(var_ready[layer], passes)
                act.activation(std[:, :], var[:, :], ACT.Sqrt).then_inc(std_ready[layer], 1)

            def normalise(layer):
                passes = 1 if layer else 3
                row_std(layer, passes)
                act.wait_ge(norm_ready[layer], passes)
                with act.Fori(0, T) as t:
                    act.wait_ge(h_stored[layer], t + 1)
                    act.activation(h_tile[:, :], row_tile(xs, t), ACT.Relu, bias=shift[:, bass.ds(t, 1)],
                                   scale=rstd[:, bass.ds(t, 1)]).then_inc(h_ready[layer], 1)

            def finish(layer, n):
                if layer == 1:
                    act.wait_ge(hid_ready[layer], n + 1)
                    act.activation(hid_tile[:, :], ps_f[:, 0:P], ACT.Relu, bias=b1_col[:, :]).then_inc(hid_copied[layer], 1)
                if layer == 3:
                    act.wait_ge(elu_in[layer], n + 1)
                    act.activation(hid_tile[:, :], sum_tile[:, :], ACT.Exp).then_inc(elu_exp[layer], 1)

            def attend(layer, t, scores, probs):
                act.wait_ge(rowmax_ready[layer], t + 1)
                act.activation(probs, scores, ACT.Exp, bias=negmax[:, :],
                               accum_out=denom[:, :]).then_inc(probs_ready[layer], 1)
                for c in range(CH):
                    act.wait_ge(pT_ready[layer], t * CH + c + 1)
                    if c >= 2:
                        act.wait_ge(pv_done[layer], t * CH + c - 1)
                    act.activation(pT[:, c % 2, :], ps_big[:, 2 + c % 2, :], ACT.Copy).then_inc(pT_copied[layer], 1)

            row_std(0)
            act.wait_ge(norm_ready[0], 1)
            for t in range(T):
                act.activation(hs[:, t, :], xs[:, t, :], ACT.Relu, bias=shift[:, t:t + 1],
                               scale=rstd[:, t:t + 1]).then_inc(table0_ready, 1)
            act.wait_ge(weights_in, WEIGHTS)
            act.wait_ge(consts_ready, 5)
            for i, (w, columns) in enumerate(((wq, D), (wk, D), (w3, D), (a_cols, 2), (head_cols, HEADS), (head_bias, HEADS))):
                act.activation(hT[:, i * D:i * D + columns], w[:, 0:columns], ACT.Square,
                               accum_out=weight_squares[:, i:i + 1]).then_inc(weights_squared, 1)
            def halve(t, b, half):
                act.wait_ge(scan_in[b], 16 * (half + 1))
                act.wait_ge(keys_made, t - 1)
                act.activation(halves[b], adj_bufs[:, b, :], ACT.Copy).then_inc(halves_ready, 1)

            def square(t, b):
                act.activation(square_out, adj_bufs[:, b, :], ACT.Square, bias=minus_half[:, :],
                               accum_out=square_sums[:, bass.ds(t, 1)]).then_inc(squares_done, 1)
                act.wait_ge(squares_done, t + 1)

            act.wait_ge(halves_ready, 2)
            for t in range(2):
                square(t, t)
            with act.Fori(1, T // 2) as half:
                for b in range(2):
                    halve(2 * half + b, b, half)
                    square(2 * half + b, b)

            row_std(0, 2)
            act.wait_ge(norm_ready[0], 2)
            act.wait_ge(tables_in, 16 * 4)
            for t in range(T):
                act.activation(hs[:, t, :], xs_early[:, t, :], ACT.Relu, bias=shift[:, t:t + 1],
                               scale=rstd[:, t:t + 1]).then_inc(finished_ready, 1)

            def dense():
                normalise(0)
                for layer in range(1, LAYERS):
                    normalise(layer)
                    with act.Fori(0, T) as t:
                        attend(layer, t, scores, probs)
                        finish(layer, t)

            def load_exp():
                act.activation(unused[:, :], eps_col[:, :], ACT.Exp)

            def sparse():
                row_std(0, 3)
                act.wait_ge(norm_ready[0], 3)
                act.wait_ge(tables_in, 16 * 5)
                for layer in range(LAYERS):
                    following = layer + 1
                    if layer == 1:
                        attend(layer, 0, zero_scores, zero_probs)

                    def row_h(t, b):
                        if following == LAYERS:
                            return
                        act.wait_ge(row_norm_ready[layer], t + 1)
                        if later(t):
                            act.wait_ge(rowT_ready[layer], t - 1)
                            if following != 3:
                                act.wait_ge(row_used[layer], t - 1)
                        act.activation(h_s[:, b, 0:D], row_tile(xs, t), ACT.Relu, bias=shift_s[:, b, :],
                                       scale=rstd_s[:, b, :]).then_inc(row_ready[layer], 1)
                        if following != 2:
                            act.wait_ge(rowT_ready[layer], t + 1)
                            act.activation(hT_s[:, b, :], ps_hT[:, 0:P], ACT.Copy).then_inc(rowT_copied[layer], 1)
                            act.wait_ge(row_q_ready[layer], t + 1)
                            if following == 1:
                                act.activation(row_tile(q_rows, t), ps_t[:, 0:P], ACT.Copy)\
                                    .then_inc(q_copied[layer], 1)
                            else:
                                act.activation(f1_rows[:, bass.ds(t, 1)], ps_t[:, 0:1], ACT.Copy)
                                act.activation(h_s[:, b, D:D + 1], ps_t[:, 1:2], ACT.Copy)\
                                    .then_inc(q_copied[layer], 1)

                    def row_deviation(t, b):
                        if following == LAYERS:
                            return
                        act.wait_ge(bn_ready[layer], t + 1)
                        act.activation(std_s[:, b, :], mv_s[:, b, 1:2], ACT.Sqrt,
                                       bias=eps_col[:, :]).then_inc(row_std_ready[layer], 1)
                        if layer:
                            load_exp()

                    def body(t, b, half, slots, done):
                        first = isinstance(t, int) and t == 0
                        if layer:
                            act.wait_ge(sparse_scores[layer], t + 1)
                            act.activation(prob_s[:, b, 0:slots], score_s[:, b, 0:slots], ACT.Exp, bias=negmax_s[:, b, :],
                                           accum_out=denom_s[:, b, :]).then_inc(sparse_probs[layer], 1)
                        if layer == 0:
                            row_deviation(t, b)
                        if not first and layer in (1, 2):
                            row_deviation(t - 1, 1 - b)
                        if not first and layer != 1:
                            row_h(t - 1, 1 - b)
                        if layer == 0:
                            share = (T - LONGER) // LONGER
                            for other in range(LONGER + t * share, LONGER + (t + 1) * share):
                                act.activation(hs[:, other, :], xs[:, other, :], ACT.Relu, bias=shift[:, other:other + 1],
                                               scale=rstd[:, other:other + 1]).then_inc(finished_ready, 1)
                        if layer in (1, 3):
                            act.wait_ge(uT_ready[layer], t + 1)
                            act.activation(uT_s[:, b, :], ps_uT[:, 0:P], ACT.Copy).then_inc(uT_copied[layer], 1)
                        if not first and layer == 1:
                            row_h(t - 1, 1 - b)
                        if layer == 1:
                            act.wait_ge(hid_ready[layer], t + 1)
                            act.activation(hid_s[:, b, :], ps_hid[:, 0:P], ACT.Relu,
                                           bias=b1_col[:, :]).then_inc(hid_copied[layer], 1)
                        if layer == 3:
                            act.wait_ge(delta_ready[layer], t + 1)
                            act.activation(hid_s[:, b, :], ps_delta[:, 0:P], ACT.Exp).then_inc(elu_exp[layer], 1)

                    over_tiles(body, lambda count, first, slots: act.Fori(first, first + count), T, layer)
                    tiles = LONGER if layer == 0 else T
                    if layer:
                        row_deviation(tiles - 1, 1)
                    row_h(tiles - 1, 1)
                    if layer == 0:
                        for n in range((T - LONGER) // 4):
                            act.wait_ge(row_q_ready[0], tiles + n + 1)
                            act.activation(q_rows[:, tiles + 4 * n:tiles + 4 * n + 4, :].rearrange("p t d -> p (t d)"),
                                           ps_big[:, 2 + (n + 1) % 2, :], ACT.Copy).then_inc(q_copied[0], 1)

            act.wait_ge(flag_ready, 1)
            bad = act.value_load(bad_flag[0:1, 0:1])
            with act.If(bad > 0):
                dense()
            with act.Else():
                sparse()

        @block.vector
        def _(dve):
            step = Chain(dve, dve_step)

            def row_tile(a, t):
                return a[:, bass.ds(t, 1), :].rearrange("p o d -> p (o d)")

            def weight_products():
                dve.wait_ge(ident_ready, 3)
                dve.wait_ge(wT_ready, 1)
                dve.tensor_copy(wT[:, :, :].rearrange("p a d -> p (a d)"), ps_t[:, :]).then_inc(wT_copied, 1)
                dve.wait_ge(products_ready, 1)
                step(dve.tensor_copy(w_qk[:, :], ps_e[:, 0:D]))
                step(dve.tensor_copy(w_v1[:, :], ps_acc[:, 0:D]))
                step(dve.tensor_copy(w_a[:, :], ps_f[:, 0:2]))
                dve.tensor_scalar(w_a2[:, :], ones[:, :], w_a[:, 1:2], None, ALU.mult).then_inc(products_copied, 1)
                dve.wait_ge(consts_ready, 5)
                step(dve.tensor_copy(totals[:, :], ps_f[:, 64:72]))
                step(dve.tensor_tensor(small[:, 0:1], totals[:, 0:1], totals[:, 1:2], ALU.mult))
                step(dve.tensor_tensor(small[:, 1:2], totals[:, 2:3], totals[:, 3:4], ALU.mult))
                qk_limit = ((NEG_BIG - 200.0) / (2 * D)) ** 2
                for i, (col, limit) in enumerate(((small[:, 0:1], qk_limit), (small[:, 1:2], 1e20),
                                                  (totals[:, 4:5], 1e20), (totals[:, 5:6], 1e20))):
                    step(dve.tensor_scalar(bad_cols[:, i:i + 1], col, limit, 0.0, ALU.is_lt, ALU.is_equal))

            def layer_stats(layer, passes=1):
                even_mean, even_m2, odd_mean, odd_m2 = (stats[:, :, i] for i in (1, 2, 4, 5))
                step(dve.tensor_tensor(mean[:, :], even_mean, odd_mean, ALU.add))
                step(dve.tensor_tensor(gap[:, :], even_mean, odd_mean, ALU.subtract))
                step(dve.tensor_tensor(var[:, :], even_m2, odd_m2, ALU.add))
                step(dve.tensor_tensor(gap[:, :], gap[:, :], gap[:, :], ALU.mult))
                step(dve.scalar_tensor_tensor(out=var[:, :], in0=gap[:, :], scalar=D / 4.0, in1=var[:, :],
                                              op0=ALU.mult, op1=ALU.add))
                dve.tensor_scalar(var[:, :], var[:, :], 1.0 / D, LN_EPS, ALU.mult, ALU.add).then_inc(var_ready[layer], 1)
                dve.wait_ge(std_ready[layer], passes)
                step(dve.reciprocal(rstd[:, :], std[:, :]))
                dve.scalar_tensor_tensor(out=shift[:, :], in0=mean[:, :], scalar=-0.5, in1=rstd[:, :],
                                         op0=ALU.mult, op1=ALU.mult).then_inc(norm_ready[layer], 1)

            def row_stats():
                with dve.Fori(0, T // 8) as eighth:
                    for i in range(8):
                        dve.bn_stats(row_tile(stats, 8 * eighth + i), row_tile(xs, 8 * eighth + i)).then_inc(dve_step, 1)
                step.n = step.n + T
                dve.wait_ge(dve_step, step.n)

            def normalise(layer):
                row_stats()
                layer_stats(layer, 1 if layer else 3)
                dve.sem_inc(h_stored[layer], 1)
                with dve.Fori(0, T) as t:
                    dve.wait_ge(h_ready[layer], t + 1)
                    dve.tensor_copy(row_tile(hs, t), h_tile[:, :])
                    dve.wait_ge(hT_ready[layer], t + 1)
                    dve.tensor_copy(hT[:, bass.ds(t * P, P)], ps_t[:, 0:P]).then_inc(h_stored[layer], 1)
                    dve.wait_ge(h_stored[layer], t + 2)

            def finish(layer, n, x_tile):
                if layer == 2:
                    dve.scalar_tensor_tensor(out=x_tile, in0=u_tile[:, :], scalar=rdenom[:, :], in1=x_tile,
                                             op0=ALU.mult, op1=ALU.add).then_inc(x_updated, 1)
                    dve.wait_ge(x_updated, layer * T + n + 1)
                    return
                dve.tensor_scalar(u_tile[:, :], u_tile[:, :], rdenom[:, :], None, ALU.mult).then_inc(u_ready[layer], 1)
                dve.wait_ge(uT_ready[layer], n + 1)
                dve.tensor_copy(uT_tile[:, :], ps_e[:, 0:P]).then_inc(uT_copied[layer], 1)
                dve.wait_ge(delta_ready[layer], n + 1)
                if layer == 1:
                    step(dve.tensor_tensor(sum_tile[:, :], ps_e[:, 0:D], b2_rows[:, :], ALU.add))
                    dve.scalar_tensor_tensor(out=x_tile, in0=sum_tile[:, :], scalar=0.0, in1=x_tile,
                                             op0=ALU.max, op1=ALU.add).then_inc(x_updated, 1)
                else:
                    dve.tensor_scalar(sum_tile[:, :], ps_f[:, 0:D], 0.0, None, ALU.min).then_inc(elu_in[layer], 1)
                    dve.wait_ge(elu_exp[layer], n + 1)
                    step(dve.tensor_scalar(hid_tile[:, :], hid_tile[:, :], -1.0, None, ALU.add))
                    step(dve.scalar_tensor_tensor(out=sum_tile[:, :], in0=ps_f[:, 0:D], scalar=0.0,
                                                  in1=hid_tile[:, :], op0=ALU.max, op1=ALU.add))
                    dve.tensor_tensor(x_tile, x_tile, sum_tile[:, :], ALU.add).then_inc(x_updated, 1)
                dve.wait_ge(x_updated, layer * T + n + 1)

            def search(t, b, half, multiply=True, rank=True, early=True):
                c = 1 - b
                quarter = N // 4
                tops = [top24[:, c, i * TOP:(i + 1) * TOP] for i in range(SLOTS // TOP)]

                found = cand[:, c, 0, :]

                def multiply_part(i):
                    if multiply:
                        part = slice(i * quarter, (i + 1) * quarter)
                        return dve.tensor_tensor(key[:, part], halves[b][:, part], iota_g[:, part], ALU.mult)

                def top(*groups):
                    if multiply:
                        for g in groups:
                            last = dve.max(cand[:, b, 0, g * TOP:(g + 1) * TOP], key[:, g * GROUP:(g + 1) * GROUP])
                        return last

                def rank_step(make, after):
                    if rank:
                        if after is not None:
                            wait_alone(dve, dve_step, after, dve_passed)
                        return step.mark(make())

                dve.wait_ge(dve_step, step.n)
                if multiply:
                    dve.wait_ge(halves_ready, t + 1)
                    multiply_part(0)
                if rank:
                    dve.wait_ge(dve_step, step.n)
                    dve.tensor_reduce(group_full[:, bass.ds(t - 1, 1)], cand[:, c, 0, TOP - 1:G8:TOP], AX.X, ALU.max)
                n = rank_step(lambda: dve.scalar_tensor_tensor(out=offset[:, :], in0=found, scalar=0.0, in1=group_first[:, :],
                                                               op0=ALU.is_gt, op1=ALU.mult), None)
                multiply_part(1)
                n = rank_step(lambda: dve.tensor_tensor(found, found, offset[:, :], ALU.add), n)
                multiply_part(2)
                n = rank_step(lambda: dve.max(tops[0], found), n)
                if multiply:
                    multiply_part(3).then_inc(keys_made, 1)
                n = rank_step(lambda: dve.match_replace(cand[:, c, 1, :], tops[0], found, 0.0), n)
                if multiply:
                    wait_alone(dve, keys_made, t + 1, dve_passed)
                top(0)
                n = rank_step(lambda: dve.max(tops[1], cand[:, c, 1, :]), n)
                top(1)
                n = rank_step(lambda: dve.match_replace(found, tops[1], cand[:, c, 1, :], 0.0), n)
                top(2, 3)
                n = rank_step(lambda: dve.max(tops[2], found), n)
                if early:
                    dve.wait_ge(early_in[c], 16 * EARLY * (half + (b - 1)))
                    dve.tensor_reduce(row_tile(early_max, t - 3), early_rows[:, c, :, :].rearrange("p k d -> p d k"),
                                      AX.X, ALU.max).then_inc(early_used, 1)
                if rank:
                    dve.wait_ge(dve_step, n)
                    dve.tensor_scalar(early_slots[:, c, :], top24[:, c, :], 0.0, float(N), ALU.max, ALU.min)\
                        .then_inc(early_found, 1)
                    step.mark(dve.tensor_scalar(rows[:, bass.ds(t - 1, 1), 0:SLOTS].rearrange("p o k -> p (o k)"),
                                                top24[:, c, :], 0.0, float(N), ALU.max, ALU.min))
                if multiply:
                    step.mark(top(4, 5, 6, 7))

            def find_neighbours():
                for t in range(2):
                    dve.wait_ge(scan_in[t], 16)
                    dve.tensor_copy(halves[t], adj_bufs[:, t, :]).then_inc(halves_ready, 1)
                dve.wait_ge(iota_ready, 3)
                dve.sem_inc(early_used, 2)
                for t in range(4):
                    search(t, t % 2, t // 2, rank=t >= 1, early=t >= 3)
                weight_products()
                with step.loop(T // 2 - 2, 18, 2) as half:
                    for b in range(2):
                        search(2 * half + b, b, half)
                search(T, 0, T // 2, multiply=False)
                dve.wait_ge(dve_step, step.n)

            def sort_rows():
                by_slot = filled.rearrange("p (t k) -> p t k", k=SLOTS)
                step(dve.tensor_scalar(by_slot, rows[:, :, 0:SLOTS], 0.0, None, ALU.is_gt))
                step(dve.tensor_reduce(degree[:, :], by_slot, AX.X, ALU.add))
                dve.wait_ge(classes_ready, 1)
                step(dve.tensor_tensor(onehot.rearrange("p (c t) -> p c t", t=T),
                                       class_iota.rearrange("p (c t) -> p c t", t=T),
                                       degree[:, :].unsqueeze(1).to_broadcast([P, C, T]), ALU.is_equal))
                dve.tensor_copy(onehot_b[:, :], onehot).then_inc(onehot_ready, 1)
                dve.wait_ge(prefix_ready, 1)
                h2 = CT // 2
                step(dve.tensor_copy(class_total.rearrange("p (a b) -> p a b", a=2), ps_big[:, 2:4, 0:h2]))
                src, n, reach = class_total, 0, 1
                while reach < CT:
                    dst = run_sum[n % 2]
                    dve.tensor_copy(dst[:, 0:reach], src[:, 0:reach])
                    step(dve.tensor_tensor(dst[:, reach:], src[:, reach:], src[:, 0:CT - reach], ALU.add))
                    src, n, reach = dst, n + 1, 2 * reach
                step(dve.tensor_tensor(src, src, class_total, ALU.subtract))
                places = run_sum[n % 2]
                step(dve.tensor_tensor(places.rearrange("p (a b) -> p a b", a=2), src.rearrange("p (a b) -> p a b", a=2),
                                       ps_big[:, 0:2, 0:h2], ALU.add))
                step(dve.tensor_tensor(places, places, onehot, ALU.mult))
                step(dve.tensor_reduce(place[:, :], places.rearrange("p (c t) -> p t c", t=T), AX.X, ALU.add))
                dve.tensor_copy(place_u[:, :], place[:, :]).then_inc(places_ready, 1)
                for t in range(T + 1, T + 3):
                    search(t, t % 2, t // 2, multiply=False, rank=False)
                dve.wait_ge(early_used, T + 2)
                step(dve.tensor_tensor(xs_early, xs, early_max, ALU.add))
                step(dve.tensor_scalar(hs_rows[:, :, D], place[:, :], 1.0, None, ALU.add))
                for t in range(T):
                    step.mark(dve.bn_stats(stats[:, t, :], xs_early[:, t, :]))
                dve.wait_ge(dve_step, step.n)
                layer_stats(0, 2)
                step(dve.tensor_reduce(bad_cols[:, 4:5], group_full[:, :], AX.X, ALU.max))
                step(dve.tensor_reduce(bad_cols[:, 5:6], onehot[:, 0:T], AX.X, ALU.max))
                dve.wait_ge(squares_done, T)
                step(dve.tensor_scalar(square_sums[:, :], square_sums[:, :], N / 4.0, None, ALU.not_equal))
                step(dve.tensor_reduce(bad_cols[:, 6:7], square_sums[:, :], AX.X, ALU.max))
                for i, (first, slots) in enumerate(RUNS):
                    longer = src[:, (SLOTS - slots) * T:(SLOTS - slots) * T + 1]
                    step(dve.tensor_scalar(bad_cols[:, 7 + i:8 + i], longer, float(first * P), None, ALU.is_gt))
                step(dve.tensor_scalar(bad_cols[:, 7 + len(RUNS):8 + len(RUNS)], src[:, SLOTS * T:SLOTS * T + 1],
                                       float((T - 1) * P), None, ALU.is_lt))
                step(dve.tensor_scalar(bad_cols[:, :], bad_cols[:, :], 0.0, None, ALU.is_gt))
                dve.tensor_reduce(bad_col[:, :], bad_cols[:, :], AX.X, ALU.add).then_inc(bad_ready, 1)
                dve.wait_ge(bad_summed, 1)
                dve.tensor_copy(bad_flag[:, :], ps_f[:, 0:1]).then_inc(flag_ready, 1)

            def dense_scores(layer, t):
                hT_tile = hT[:, bass.ds(t * P, P)]
                banks = CH * heads[layer]
                if layer == 1:
                    dve.wait_ge(lhs_product[layer], t + 1)
                    dve.tensor_copy(queries[:, 0, :], ps_t[:, 0:P]).then_inc(lhs_ready[layer], 1)
                    dve.wait_ge(adj_in, 16 * (layer * T + t + 1))
                    step(dve.tensor_scalar(scores, adj_tile, 0.0, -NEG_BIG, ALU.is_le, ALU.mult))
                    for c in range(CH):
                        part = scores[:, c * 512:(c + 1) * 512]
                        dve.wait_ge(banks_ready[layer], t * banks + c + 1)
                        dve.tensor_tensor(part, part, ps_big[:, c % 2, :], ALU.add).then_inc(banks_used[layer], 1)
                    dve.wait_ge(banks_used[layer], (t + 1) * banks + 2)
                if layer == 2:
                    for k in range(HEADS):
                        ins = dve.tensor_scalar(queries[:, k, :], hT_tile, head_cols[:, k:k + 1], None, ALU.mult)
                    ins.then_inc(lhs_ready[layer], 1)
                    dve.wait_ge(adj_in, 16 * (layer * T + t + 1))
                    step(dve.tensor_scalar(scores, adj_tile, 1.0, None, ALU.is_ge))
                    step(dve.scalar_tensor_tensor(out=scores, in0=adj_tile, scalar=float(HEADS),
                                                  in1=scores, op0=ALU.is_le, op1=ALU.mult))
                    step(dve.tensor_scalar(scores, scores, -1.0, -NEG_INF, ALU.add, ALU.mult))
                    for i in range(banks):
                        c, k = divmod(i, HEADS)
                        part = scores[:, c * 512:(c + 1) * 512]
                        dve.wait_ge(banks_ready[layer], t * banks + i + 1)
                        dve.tensor_scalar(chunk_b[:, :], ps_big[:, i % 2, :], head_bias[:, k:k + 1], None,
                                          ALU.add).then_inc(banks_used[layer], 1)
                        dve.wait_ge(banks_used[layer], t * banks + i + 3)
                        step(dve.scalar_tensor_tensor(out=chunk_a[:, 0:512], in0=chunk_b[:, :], scalar=SLOPE,
                                                      in1=chunk_b[:, :], op0=ALU.mult, op1=ALU.max))
                        step(dve.scalar_tensor_tensor(out=chunk_b[:, :], in0=adj_tile[:, c * 512:(c + 1) * 512],
                                                      scalar=float(k + 1), in1=chunk_a[:, 0:512],
                                                      op0=ALU.is_equal, op1=ALU.mult))
                        step(dve.tensor_tensor(part, part, chunk_b[:, :], ALU.add))
                if layer == 3:
                    dve.tensor_copy(queries[:, 0, :], hT_tile).then_inc(lhs_made[layer], 1)
                    dve.wait_ge(lhs_product[layer], t + 1)
                    dve.tensor_copy(f1_col[:, :], ps_t[:, 0:1]).then_inc(lhs_ready[layer], 1)
                    dve.wait_ge(lhs_ready[layer], t + 1)
                    dve.wait_ge(adj_in, 16 * (layer * T + t + 1))
                    step(dve.tensor_scalar(scores, adj_tile, 0.0, NEG_INF, ALU.is_le, ALU.mult))
                    for c in range(CH):
                        part = scores[:, c * 512:(c + 1) * 512]
                        dve.wait_ge(banks_ready[layer], t * banks + c + 1)
                        dve.tensor_scalar(chunk_b[:, :], ps_big[:, c % 2, :], f1_col[:, :], None,
                                          ALU.add).then_inc(banks_used[layer], 1)
                        dve.wait_ge(banks_used[layer], t * banks + c + 3)
                        step(dve.scalar_tensor_tensor(out=chunk_a[:, 0:512], in0=chunk_b[:, :], scalar=SLOPE,
                                                      in1=chunk_b[:, :], op0=ALU.mult, op1=ALU.max))
                        step(dve.scalar_tensor_tensor(out=chunk_b[:, :], in0=adj_tile[:, c * 512:(c + 1) * 512],
                                                      scalar=0.0, in1=chunk_a[:, 0:512], op0=ALU.is_gt, op1=ALU.mult))
                        step(dve.tensor_tensor(part, part, chunk_b[:, :], ALU.add))

            def dense():
                dve.wait_ge(x_again, 16)
                normalise(0)
                dve.sem_inc(quarters_used, 2)
                with step.loop(T, P * Q) as t:
                    dve.wait_ge(adj_in, 16 * (t + 1))
                    dve.tensor_scalar(mask_b, adj_tile, 0.0, None, ALU.not_equal).then_inc(mask_ready, 1)
                    dve.wait_ge(mask_ready, t + 1)
                    dve.sem_inc(adj_free, 1)
                    with step.loop(P, Q) as r:
                        for q in range(Q):
                            dve.wait_ge(quarters_ready, (t * P + r) * Q + q + 1)
                            dve.tensor_tensor(chunk_a[:, :],
                                              ps_big[:, 2 * (q % 2):2 * (q % 2) + 2, :].rearrange("p a b -> p (a b)"),
                                              hT[:, q * 1024:(q + 1) * 1024], ALU.mult).then_inc(quarters_used, 1)
                            dve.wait_ge(quarters_used, (t * P + r) * Q + q + 3)
                            step(dve.tensor_reduce(quarter_max[:, q:q + 1], chunk_a[:, :], AX.X, ALU.max))
                        dve.tensor_reduce(maxT[:, bass.ds(r, 1)], quarter_max[:, :], AX.X, ALU.max).then_inc(row_max_taken, 1)
                        dve.wait_ge(row_max_taken, t * P + r + 1)
                    dve.sem_inc(maxT_ready, 1)
                    dve.wait_ge(max_ready, t + 1)
                    dve.tensor_tensor(row_tile(xs, t), row_tile(xs, t), ps_t[:, 0:P], ALU.add).then_inc(x_updated, 1)
                    dve.wait_ge(x_updated, t + 1)

                STEPS = [0, 1 + 1, 3 + 3 * CH * HEADS + 1, 1 + 3 * CH + 1]
                FINISH = [0, 1, 0, 2]
                for layer in range(1, LAYERS):
                    normalise(layer)
                    dve.sem_inc(banks_used[layer], 2)
                    with step.loop(T, STEPS[layer] + FINISH[layer] + 1) as t:
                        dense_scores(layer, t)
                        step(dve.tensor_reduce(max_col[:, :], scores, AX.X, ALU.max))
                        dve.tensor_scalar(negmax[:, :], max_col[:, :], -1.0, None, ALU.mult).then_inc(rowmax_ready[layer], 1)
                        dve.sem_inc(adj_free, 1)
                        dve.wait_ge(probs_ready[layer], t + 1)
                        step(dve.reciprocal(rdenom[:, :], denom[:, :]))
                        dve.wait_ge(pv_done[layer], (t + 1) * CH)
                        dve.tensor_copy(u_tile[:, :], ps_acc[:, 0:D]).then_inc(u_copied[layer], 1)
                        dve.wait_ge(u_copied[layer], t + 1)
                        finish(layer, t, row_tile(xs, t))

            def sparse():
                dve.wait_ge(rows_sorted, 16)
                full = filled.rearrange("p (t k) -> p t k", k=SLOTS)
                step(dve.tensor_scalar(full, rows[:, :, 0:SLOTS], 0.0, None, ALU.is_gt))
                step(dve.tensor_scalar(pad_bias[:, :, :], full, -PAD_BIAS, PAD_BIAS, ALU.mult, ALU.add))
                step(dve.tensor_scalar(no_nbr[:, :], full[:, :, 0], -1.0, 1.0, ALU.mult, ALU.add))
                step(dve.tensor_tensor(xs[:, LONGER:, :], xs[:, LONGER:, :], early_max[:, LONGER:, :], ALU.add))
                for t in range(LONGER, T):
                    step.mark(dve.bn_stats(stats[:, t, :], xs[:, t, :]))
                dve.wait_ge(dve_step, step.n)
                layer_stats(0, 3)
                for layer in range(LAYERS):
                    following = layer + 1
                    width = widths[layer]
                    if layer == 1:
                        dve.wait_ge(lhs_product[layer], 1)
                        dve.tensor_copy(queries[:, 0, :], ps_t[:, 0:P]).then_inc(lhs_ready[layer], 1)
                        dve.sem_inc(banks_used[layer], 2)
                        for c in range(CH):
                            dve.wait_ge(banks_ready[layer], c + 1)
                            dve.tensor_scalar(zero_scores[:, c * 512:(c + 1) * 512], ps_big[:, c % 2, :], -NEG_BIG, None,
                                              ALU.add).then_inc(banks_used[layer], 1)
                        dve.wait_ge(banks_used[layer], CH + 2)
                        dve.tensor_reduce(negmax[:, :], zero_scores, AX.X, ALU.max, negate=True)\
                            .then_inc(rowmax_ready[layer], 1)
                        dve.wait_ge(probs_ready[layer], 1)
                        step(dve.reciprocal(rdenom[:, :], denom[:, :]))
                        dve.wait_ge(pv_done[layer], CH)
                        dve.tensor_scalar(zero_row[:, :], ps_acc[:, 0:D], rdenom[:, :], None, ALU.mult)\
                            .then_inc(zero_ready, 1)
                        dve.wait_ge(zero_ready, 1)
                    if layer >= 2:
                        dve.wait_ge(rowT_ready[layer - 1], T)
                        step(dve.tensor_scalar(zero_row[:, :], ps_acc[:, 0:D], 1.0 / N, None, ALU.mult))

                    def gathered_rows(b, slots):
                        return gathered[b][:, 0:slots * width].rearrange("p (k w) -> p k w", w=width)

                    stores, stored_before = ((scattered, 0), (written, 0), (written, T // 2), (scattered, LONGER // 2))[layer]

                    def gather_done(t):
                        return t + 1 + tiles_before(layer, T)

                    def node_of(t):
                        return rows[:, bass.ds(t, 1), W_NODE:W_NODE + 1].rearrange("p o k -> p (o k)")

                    def maximum(t, b, slots, done):
                        dve.wait_ge(gather_in[b], 16 * done)
                        dve.tensor_reduce(sum_s[:, b, :], gathered_rows(b, slots).rearrange("p k d -> p d k"), AX.X, ALU.max)\
                            .then_inc(gather_used, 1)
                        dve.wait_ge(gather_used, gather_done(t))
                        step(dve.tensor_tensor(sum_s[:, b, :], sum_s[:, b, :], row_tile(early_max, t), ALU.max))
                        step(dve.tensor_tensor(row_tile(xs, t), row_tile(xs, t), sum_s[:, b, :], ALU.add), dve_passed)

                    def score(t, b, slots, done, first_gap, second_gap):
                        g = gathered_rows(b, slots)[:, :, 0:D]
                        sc, tmp, bias = score_s[:, b, 0:slots], prob_s[:, b, 0:slots], row_tile(pad_bias, t)[:, 0:slots]
                        dve.wait_ge(gather_in[b], 16 * done)
                        if layer == 3:
                            step(dve.scalar_tensor_tensor(out=tmp, in0=gathered_rows(b, slots)[:, :, D], scalar=f1_rows[:, bass.ds(t, 1)],
                                                          in1=bias, op0=ALU.add, op1=ALU.add))
                        else:
                            w = weighted[:, 0:slots * D].rearrange("p (k d) -> p k d", d=D)
                            n = step.mark(dve.tensor_tensor(w, g, q_rows[:, bass.ds(t, 1), :].to_broadcast([P, slots, D]),
                                                            ALU.mult))
                            first_gap()
                            dve.wait_ge(dve_step, n)
                            n = step.mark(dve.tensor_reduce(sc, w, AX.X, ALU.add))
                            second_gap()
                            dve.wait_ge(dve_step, n)
                            if layer == 2:
                                step(dve.scalar_tensor_tensor(out=tmp, in0=sc, scalar=head_bias[:, 0:1], in1=bias,
                                                              op0=ALU.add, op1=ALU.add))
                            else:
                                step(dve.tensor_tensor(sc, sc, bias, ALU.add))
                        if layer >= 2:
                            step(dve.scalar_tensor_tensor(out=sc, in0=tmp, scalar=SLOPE, in1=tmp, op0=ALU.mult, op1=ALU.max))
                        dve.tensor_reduce(negmax_s[:, b, :], sc, AX.X, ALU.max, negate=True).then_inc(sparse_scores[layer], 1)

                    def weigh(t, b, slots, first_gap, second_gap):
                        g = gathered_rows(b, slots)[:, :, 0:D]
                        w = weighted[:, 0:slots * D].rearrange("p (k d) -> p k d", d=D)
                        dve.wait_ge(sparse_probs[layer], t + 1)
                        n = step.mark(dve.reciprocal(rdenom_s[:, b, :], denom_s[:, b, :]))
                        dve.tensor_tensor(w, g, prob_s[:, b, 0:slots].unsqueeze(2).to_broadcast([P, slots, D]), ALU.mult)\
                            .then_inc(gather_used, 1)
                        first_gap()
                        dve.wait_ge(gather_used, gather_done(t))
                        m = step.mark(dve.tensor_reduce(sum_s[:, b, :], w.rearrange("p k d -> p d k"), AX.X, ALU.add))
                        second_gap()
                        dve.wait_ge(dve_step, m)
                        last = isinstance(t, int) and t == T - 1
                        if layer == 2:
                            x_tile = row_tile(xs, t)
                            if last:
                                step(dve.scalar_tensor_tensor(out=x_tile, in0=zero_row[:, :], scalar=no_nbr[:, bass.ds(t, 1)],
                                                              in1=x_tile, op0=ALU.mult, op1=ALU.add))
                            step.mark(dve.scalar_tensor_tensor(out=x_tile, in0=sum_s[:, b, :], scalar=rdenom_s[:, b, :],
                                                               in1=x_tile, op0=ALU.mult, op1=ALU.add))
                        elif last:
                            step(dve.tensor_scalar(sum_s[:, b, :], sum_s[:, b, :], rdenom_s[:, b, :], None, ALU.mult))
                            dve.scalar_tensor_tensor(out=u_s[:, b, :], in0=zero_row[:, :], scalar=no_nbr[:, bass.ds(t, 1)],
                                                     in1=sum_s[:, b, :], op0=ALU.mult, op1=ALU.add).then_inc(u_ready[layer], 1)
                        else:
                            dve.tensor_scalar(u_s[:, b, :], sum_s[:, b, :], rdenom_s[:, b, :], None, ALU.mult)\
                                .then_inc(u_ready[layer], 1)

                    def update(t, b):
                        dve.wait_ge(delta_ready[layer], t + 1)
                        step(dve.tensor_tensor(sum_d[:, :], ps_delta[:, 0:D], b2_rows[:, :], ALU.add))
                        step.mark(dve.scalar_tensor_tensor(out=row_tile(xs, t), in0=sum_d[:, :], scalar=0.0,
                                                           in1=row_tile(xs, t), op0=ALU.max, op1=ALU.add))

                    def row_moments(t, b):
                        wait_alone(dve, dve_step, step.n, dve_passed)
                        step.mark(dve.bn_stats(bn_s[:, b, :], row_tile(xs, t)))

                    def moments_joined(b):
                        wait_alone(dve, dve_step, step.n, dve_passed)
                        dve.bn_aggr(mv_s[:, b, :], bn_s[:, b, :]).then_inc(bn_ready[layer], 1)

                    def row_rstd(t, b):
                        dve.wait_ge(row_std_ready[layer], t + 1)
                        step.mark(dve.reciprocal(rstd_s[:, b, :], std_s[:, b, :]))

                    def row_shift(t, b, before_it):
                        if later(t):
                            dve.wait_ge(stores[b], 16 * (before_it + stored_before))
                        if layer == 0:
                            dve.tensor_copy(node_s[:, b, :], node_of(t))
                            dve.tensor_copy(h_s[:, b, D:D + 1], place_no[:, bass.ds(t, 1)])
                        dve.wait_ge(dve_step, step.n)
                        dve.scalar_tensor_tensor(out=shift_s[:, b, :], in0=mv_s[:, b, 0:1], scalar=-1.0,
                                                 in1=rstd_s[:, b, :], op0=ALU.mult, op1=ALU.mult)\
                            .then_inc(row_norm_ready[layer], 1)

                    def output(t, b, before_it):
                        dve.wait_ge(elu_exp[layer], t + 1)
                        step(dve.tensor_scalar(hid_s[:, b, :], hid_s[:, b, :], 1.0, -1.0, ALU.min, ALU.add))
                        step(dve.scalar_tensor_tensor(out=sum_s[:, b, :], in0=ps_delta[:, 0:D], scalar=0.0, in1=hid_s[:, b, :],
                                                      op0=ALU.max, op1=ALU.add))
                        if later(t):
                            dve.wait_ge(stores[b], 16 * (before_it + stored_before))
                        dve.tensor_scalar(node_s[:, b, :], node_of(t), -1.0, None, ALU.add)
                        dve.tensor_tensor(h_s[:, b, 0:D], row_tile(xs, t), sum_s[:, b, :], ALU.add)\
                            .then_inc(final_ready[layer], 1)

                    def prepare(t, b):
                        dve.wait_ge(row_ready[layer], t + 1)
                        if layer == 0:
                            dve.tensor_copy(row_tile(hs, t), h_s[:, b, 0:D])
                            dve.wait_ge(rowT_copied[layer], t + 1)
                            dve.tensor_copy(hT[:, bass.ds(t * P, P)], ps_hT[:, 0:P]).then_inc(row_used[layer], 1)
                        if layer == 1:
                            dve.tensor_tensor(row_tile(q_rows, t), h_s[:, b, 0:D], w0_rows[:, :], ALU.mult)\
                                .then_inc(row_used[layer], 1)

                    def body(t, b, half, slots, done):
                        before, c, earlier = t - 1, 1 - b, half - 1 + b
                        do = not (isinstance(t, int) and t == 0)
                        nothing = lambda: None
                        if layer == 0:
                            maximum(t, b, slots, done)
                            row_moments(t, b)
                            moments_joined(b)
                            if do:
                                row_rstd(before, c)
                                row_shift(before, c, earlier)
                                prepare(before, c)
                        if layer == 1:
                            def places():
                                step.mark(dve.tensor_copy(rows[:, bass.ds(t, 1), 0:slots].rearrange("p o k -> p (o k)"),
                                                          gathered_rows(b, slots)[:, :, D]))
                                if later(t):
                                    prepare(t - 2, b)

                            score(t, b, slots, done, places, nothing)
                            if do:
                                update(before, c)

                            def moments():
                                row_moments(before, c)
                                moments_joined(c)

                            weigh(t, b, slots, moments if do else nothing, (lambda: row_rstd(before, c)) if do else nothing)
                            if do:
                                row_shift(before, c, earlier)
                        if layer == 2:
                            score(t, b, slots, done, (lambda: row_moments(before, c)) if do else nothing,
                                  (lambda: moments_joined(c)) if do else nothing)
                            weigh(t, b, slots, nothing, (lambda: row_rstd(before, c)) if do else nothing)
                            if do:
                                row_shift(before, c, earlier)
                        if layer == 3:
                            score(t, b, slots, done, nothing, nothing)
                            if do:
                                output(before, c, earlier)
                            weigh(t, b, slots, nothing, nothing)

                    def last_rest(t, b, earlier):
                        if layer == 1:
                            prepare(t - 1, 1 - b)
                            update(t, b)
                        if layer in (1, 2):
                            row_moments(t, b)
                            moments_joined(b)
                        if layer < 3:
                            row_rstd(t, b)
                            row_shift(t, b, earlier)
                        if layer < 2:
                            prepare(t, b)
                        if layer == 3:
                            output(t, b, earlier)

                    def loop(count, first, slots):
                        return step.loop(count, [8, 20, 18, 12][layer], first)

                    over_tiles(body, loop, T, layer)
                    tiles = LONGER if layer == 0 else T
                    last_rest(tiles - 1, 1, tiles // 2 - 1)
                    if layer == 0:
                        for n in range((T - LONGER) // 4):
                            dve.wait_ge(rowT_ready[0], tiles + n + 1)
                            at = (tiles + 4 * n) * P
                            dve.tensor_copy(hT[:, at:at + 4 * P], ps_big[:, n % 2, :]).then_inc(row_used[0], 1)

            dve.wait_ge(x_in, 16)
            row_stats()
            layer_stats(0)
            find_neighbours()
            sort_rows()
            dve.wait_ge(flag_ready, 1)
            chained = step.n
            bad = dve.value_load(bad_flag[0:1, 0:1])
            with dve.If(bad > 0):
                dense()
            step.n = chained
            with dve.Else():
                sparse()


_INS = ['x', 'adj', 'L1_gnn_Wq', 'L1_gnn_Wk', 'L1_gnn_Wv', 'L1_gnn_W1', 'L1_gnn_b1', 'L1_gnn_W2', 'L1_gnn_b2',
        'L2_gnn_W', 'L2_gnn_b', 'L3_gnn_W', 'L3_gnn_a']
_OUTS = [((4096, 128), 'float32')]


def kernel(**inputs):
    import numpy as _np
    import concourse.bacc as _bacc
    from concourse import mybir as _mybir
    from concourse.bass_utils import run_bass_kernel_spmd as _run

    nc = _bacc.Bacc("TRN2", target_bir_lowering=False, num_devices=1)
    arrays, args = {}, []
    for name in _INS:
        a = _np.ascontiguousarray(inputs[name])
        arrays[f"in_{name}_dram"] = a
        args.append(nc.dram_tensor(f"in_{name}_dram", a.shape, _mybir.dt.from_np(a.dtype), kind="ExternalInput").ap())
    for i, (shape, dtype) in enumerate(_OUTS):
        dt = _mybir.dt.from_np(_np.dtype(dtype))
        args.append(nc.dram_tensor(f"out_{i}_dram", shape, dt, kind="ExternalOutput").ap())
    build(nc, *args)
    r = _run(nc, [arrays], core_ids=[0])
    got = tuple(r.results[0][f"out_{i}_dram"] for i in range(len(_OUTS)))
    return got[0]
```
